# Optimizing a Trainium2 kernel written in Bass

```python
import numpy as np
import jax
import jax.numpy as jnp

def _softmax(x, axis=-1):
    return jax.nn.softmax(x, axis=axis)

def _gelu(x):
    return jax.nn.gelu(x, approximate=True)

def _silu(x):
    return jax.nn.silu(x)

def _sigmoid(x):
    return jax.nn.sigmoid(x)

def _layernorm(x, axis=-1, eps=1e-05):
    m = jnp.mean(x, axis=axis, keepdims=True)
    v = jnp.var(x, axis=axis, keepdims=True)
    return (x - m) / jnp.sqrt(v + eps)

def _scatter_add(tgt, idx, src, axis=0):
    return tgt.at[idx].add(src)

def _segment_sum(src, seg, n):
    return jax.ops.segment_sum(src, seg, n)
kernel_name = 'mk_adj_preln_d2_adj_r2_377561'

def setup_inputs(seed: int=0):
    np.random.seed(seed)
    _w = jnp.asarray

    def _rec_inputs():
        import jax
        import jax.numpy as jnp
        _gk = jax.random.key(seed)
        x = -0.0002037 + 1 * jax.random.normal(jax.random.fold_in(_gk, 1), (5000, 128), jnp.float32)
        _a = jax.random.bernoulli(jax.random.fold_in(_gk, 2), 0.0008, (5000, 5000))
        _af = _a.astype(jnp.float32)
        adj = _af
        return (x, adj)
    x, adj = _rec_inputs()

    def _L0_gnn_setup():
        import jax, jax.numpy as jnp
        import numpy as np
        N = 5000
        F = 128
        C = 16
        AL = 0.1
        EPS = 1e-12
        key = jax.random.key(seed)
        k1, k2, k3, k4 = jax.random.split(key, 4)
        A = (jax.random.uniform(k1, (N, N)) > 0.99).astype(jnp.float32)
        x = jax.random.normal(k2, (N, F), dtype=jnp.float32)
        h0 = jax.random.normal(k3, (N, F), dtype=jnp.float32)
        labels = jax.random.randint(k4, (N,), 0, C)
        y = jax.nn.one_hot(labels, C, dtype=jnp.float32)
        return {'input': x, 'A': A, 'h0': h0, 'y': y}
    _L0_gnn_all = _L0_gnn_setup()
    _L0_gnn_in = {k: v for k, v in _L0_gnn_all.items() if k in ('h0', 'y')}
    del _L0_gnn_all

    def _L1_gnn_setup():
        import jax, jax.numpy as jnp
        import numpy as np
        from jax import lax
        D_MODEL = 128
        D_STATE = 16
        D_CONV = 4
        EXPAND = 2
        D_INNER = EXPAND * D_MODEL
        DT_RANK = (D_MODEL + 15) // 16
        N = 2048
        EPS = 1e-05

        def _mamba(h, w_in, conv_w, conv_b, w_xp, w_dt, b_dt, A_log, D_skip, w_out):
            L = h.shape[0]
            xz = h @ w_in
            xc, z = (xz[:, :D_INNER], xz[:, D_INNER:])
            xpad = jnp.pad(xc, ((D_CONV - 1, 0), (0, 0)))
            xconv = sum((xpad[k:k + L] * conv_w[:, k] for k in range(D_CONV))) + conv_b
            u = jax.nn.silu(xconv)
            dbc = u @ w_xp
            dt = jax.nn.softplus(dbc[:, :DT_RANK] @ w_dt + b_dt)
            B = dbc[:, DT_RANK:DT_RANK + D_STATE]
            C = dbc[:, DT_RANK + D_STATE:]
            A = -jnp.exp(A_log)
            dA = jnp.exp(dt[:, :, None] * A[None])
            dBu = dt[:, :, None] * B[:, None, :] * u[:, :, None]

            def step(hst, inp):
                dAt, dBut, Ct = inp
                hst = dAt * hst + dBut
                return (hst, hst @ Ct)
            _, ys = lax.scan(step, jnp.zeros((D_INNER, D_STATE), h.dtype), (dA, dBu, C))
            y = ys + u * D_skip
            y = y * jax.nn.silu(z)
            return y @ w_out
        key = jax.random.key(seed)
        ks = jax.random.split(key, 16)
        x = jax.random.normal(ks[0], (N, D_MODEL), dtype=jnp.float32)
        a = jax.random.uniform(ks[1], (N, N), dtype=jnp.float32)
        adj = a / a.sum(axis=1, keepdims=True)
        s = lambda fi, fo: 1.0 / np.sqrt(fi)
        gcn_w = jax.random.uniform(ks[2], (D_MODEL, D_MODEL), jnp.float32, -s(D_MODEL, 0), s(D_MODEL, 0))
        gcn_b = jnp.zeros((D_MODEL,), jnp.float32)
        ln_g = jnp.ones((D_MODEL,), jnp.float32)
        ln_b = jnp.zeros((D_MODEL,), jnp.float32)
        w_in = jax.random.normal(ks[3], (D_MODEL, 2 * D_INNER), jnp.float32) * s(D_MODEL, 0)
        conv_w = jax.random.normal(ks[4], (D_INNER, D_CONV), jnp.float32) * s(D_CONV, 0)
        conv_b = jnp.zeros((D_INNER,), jnp.float32)
        w_xp = jax.random.normal(ks[5], (D_INNER, DT_RANK + 2 * D_STATE), jnp.float32) * s(D_INNER, 0)
        w_dt = jax.random.normal(ks[6], (DT_RANK, D_INNER), jnp.float32) * s(DT_RANK, 0)
        b_dt = jnp.log(jnp.expm1(jnp.exp(jax.random.uniform(ks[7], (D_INNER,), jnp.float32, np.log(0.001), np.log(0.1)))))
        A_log = jnp.log(jnp.broadcast_to(jnp.arange(1, D_STATE + 1, dtype=jnp.float32), (D_INNER, D_STATE)))
        D_skip = jnp.ones((D_INNER,), jnp.float32)
        w_out = jax.random.normal(ks[8], (D_INNER, D_MODEL), jnp.float32) * s(D_INNER, 0)
        return dict(x=x, adj=adj, gcn_w=gcn_w, gcn_b=gcn_b, ln_g=ln_g, ln_b=ln_b, w_in=w_in, conv_w=conv_w, conv_b=conv_b, w_xp=w_xp, w_dt=w_dt, b_dt=b_dt, A_log=A_log, D_skip=D_skip, w_out=w_out)
    _L1_gnn_all = _L1_gnn_setup()
    _L1_gnn_in = {k: v for k, v in _L1_gnn_all.items() if k in ('gcn_w', 'gcn_b', 'ln_g', 'ln_b', 'w_in', 'conv_w', 'conv_b', 'w_xp', 'w_dt', 'b_dt', 'A_log', 'D_skip', 'w_out')}
    del _L1_gnn_all
    return {'x': x, 'adj': adj, 'L0_gnn_h0': _L0_gnn_in['h0'], 'L0_gnn_y': _L0_gnn_in['y'], 'L1_gnn_gcn_w': _L1_gnn_in['gcn_w'], 'L1_gnn_gcn_b': _L1_gnn_in['gcn_b'], 'L1_gnn_ln_g': _L1_gnn_in['ln_g'], 'L1_gnn_ln_b': _L1_gnn_in['ln_b'], 'L1_gnn_w_in': _L1_gnn_in['w_in'], 'L1_gnn_conv_w': _L1_gnn_in['conv_w'], 'L1_gnn_conv_b': _L1_gnn_in['conv_b'], 'L1_gnn_w_xp': _L1_gnn_in['w_xp'], 'L1_gnn_w_dt': _L1_gnn_in['w_dt'], 'L1_gnn_b_dt': _L1_gnn_in['b_dt'], 'L1_gnn_A_log': _L1_gnn_in['A_log'], 'L1_gnn_D_skip': _L1_gnn_in['D_skip'], 'L1_gnn_w_out': _L1_gnn_in['w_out']}

def reference(x, adj, L0_gnn_h0, L0_gnn_y, L1_gnn_gcn_w, L1_gnn_gcn_b, L1_gnn_ln_g, L1_gnn_ln_b, L1_gnn_w_in, L1_gnn_conv_w, L1_gnn_conv_b, L1_gnn_w_xp, L1_gnn_w_dt, L1_gnn_b_dt, L1_gnn_A_log, L1_gnn_D_skip, L1_gnn_w_out):
    import jax
    import jax.numpy as jnp

    def _L0_gnn_ref(input, A, h0, y):
        import jax, jax.numpy as jnp
        import numpy as np
        N = 5000
        F = 128
        C = 16
        AL = 0.1
        EPS = 1e-12
        adj = A * (y @ y.T)
        row_l1 = jnp.maximum(jnp.sum(jnp.abs(adj), axis=1, keepdims=True), EPS)
        adj = adj / row_l1
        support = adj @ input
        return (1.0 - AL) * support + AL * h0

    def _L1_gnn_ref(x, adj, gcn_w, gcn_b, ln_g, ln_b, w_in, conv_w, conv_b, w_xp, w_dt, b_dt, A_log, D_skip, w_out):
        import jax, jax.numpy as jnp
        import numpy as np
        from jax import lax
        D_MODEL = 128
        D_STATE = 16
        D_CONV = 4
        EXPAND = 2
        D_INNER = EXPAND * D_MODEL
        DT_RANK = (D_MODEL + 15) // 16
        N = 2048
        EPS = 1e-05

        def _mamba(h, w_in, conv_w, conv_b, w_xp, w_dt, b_dt, A_log, D_skip, w_out):
            L = h.shape[0]
            xz = h @ w_in
            xc, z = (xz[:, :D_INNER], xz[:, D_INNER:])
            xpad = jnp.pad(xc, ((D_CONV - 1, 0), (0, 0)))
            xconv = sum((xpad[k:k + L] * conv_w[:, k] for k in range(D_CONV))) + conv_b
            u = jax.nn.silu(xconv)
            dbc = u @ w_xp
            dt = jax.nn.softplus(dbc[:, :DT_RANK] @ w_dt + b_dt)
            B = dbc[:, DT_RANK:DT_RANK + D_STATE]
            C = dbc[:, DT_RANK + D_STATE:]
            A = -jnp.exp(A_log)
            dA = jnp.exp(dt[:, :, None] * A[None])
            dBu = dt[:, :, None] * B[:, None, :] * u[:, :, None]

            def step(hst, inp):
                dAt, dBut, Ct = inp
                hst = dAt * hst + dBut
                return (hst, hst @ Ct)
            _, ys = lax.scan(step, jnp.zeros((D_INNER, D_STATE), h.dtype), (dA, dBu, C))
            y = ys + u * D_skip
            y = y * jax.nn.silu(z)
            return y @ w_out
        h = jax.nn.relu(adj @ x @ gcn_w + gcn_b)
        mu = h.mean(-1, keepdims=True)
        var = h.var(-1, keepdims=True)
        h = (h - mu) * lax.rsqrt(var + EPS) * ln_g + ln_b
        return _mamba(h, w_in, conv_w, conv_b, w_xp, w_dt, b_dt, A_log, D_skip, w_out)
    h = jnp.maximum(_layernorm(x, axis=-1), 0.0)
    x = x + _L0_gnn_ref(h, adj, L0_gnn_h0, L0_gnn_y)
    h = jnp.maximum(_layernorm(x, axis=-1), 0.0)
    x = x + _L1_gnn_ref(h, adj, L1_gnn_gcn_w, L1_gnn_gcn_b, L1_gnn_ln_g, L1_gnn_ln_b, L1_gnn_w_in, L1_gnn_conv_w, L1_gnn_conv_b, L1_gnn_w_xp, L1_gnn_w_dt, L1_gnn_b_dt, L1_gnn_A_log, L1_gnn_D_skip, L1_gnn_w_out)
    return x

_drawn_inputs = setup_inputs


def setup_inputs(seed=0):
    import zlib

    import numpy as np

    out = dict(_drawn_inputs(seed))
    spreads = {'L1_gnn_gcn_b': (0.0, 0.1),
     'L1_gnn_ln_g': (1.0, 0.2),
     'L1_gnn_ln_b': (0.0, 0.1),
     'L1_gnn_conv_b': (0.0, 0.1),
     'L1_gnn_D_skip': (1.0, 0.2)}
    factors = {}
    for name, (base, spread) in spreads.items():
        noise = np.random.default_rng([zlib.crc32(name.encode()), seed]).standard_normal(out[name].shape)
        drawn = base * np.exp(spread * noise) if base else spread * noise
        out[name] = jnp.asarray(drawn.astype(out[name].dtype))
    for name, factor in factors.items():
        out[name] = (out[name] * factor).astype(out[name].dtype)
    return out
```

```python
import concourse.bass as bass
from concourse import mybir
from contextlib import ExitStack

F32 = mybir.dt.float32
BF16 = mybir.dt.bfloat16
FP16 = mybir.dt.float16
U16 = mybir.dt.uint16
I32 = mybir.dt.int32
ALU = mybir.AluOpType
ACT = mybir.ActivationFunctionType

N = 5000
D = 128
P = 128
NT = -(-N // P)
NP = NT * P
CH = 512
NC = NP // CH
TPC = CH // P
HALVES = 2
HC = NC // HALVES
HW = HC * CH
HT = NT // HALVES
CLS = 16
DI = 256
CT = DI // P
ST = 16
RK = 8
KC = 4
LAST_ROWS = N - (NT - 1) * P

SLOTS = 4
GJ = HC
LPC = NT // GJ
VW = HW // 2
RING = 4
PIECE = 10

PAIRED = [3, 7, 11, 15]
OUT_STEP = 5
H_SCALE = 4096.0

LN_EPS = 1e-5
ROW_EPS = 1e-12
ALPHA = 0.1
N_WEIGHTS = 16

Y_PAIRS = [(0, 0), (0, 1), (1, 0), (1, 1), (0, 2), (2, 0), (1, 2), (2, 1)]


def build(nc, x, h0, adj_t, y_t, gcn_w, gcn_b, ln_g, ln_b, w_in, conv_w, conv_b,
          w_xp, w_dt, b_dt, a_log, d_skip, w_out, out):
    y_parts = nc.dram_tensor("y_parts", (3, CLS, NP), BF16, kind="Internal").ap()

    ctx = ExitStack()
    with ctx:
        def sb(name, shape, dt=F32):
            return ctx.enter_context(nc.sbuf_tensor(name, shape, dt))

        def sem(name):
            return ctx.enter_context(nc.semaphore(name))

        adj_ring = sb("adj_ring", [P, SLOTS, HW])
        x1 = sb("x1", [P, NT, D])
        h1 = sb("h1", [P, NT, D])
        ident = sb("ident", [P, P])
        mean_mat = sb("mean_mat", [P, P])
        ones = sb("ones", [P, 1])
        ln_eps = sb("ln_eps", [P, 1])
        sel32 = sb("sel32", [P, 2 * ST])
        sel = sb("sel", [P, 2 * ST], BF16)
        w_gcn = sb("w_gcn", [P, D])
        b_gcn = sb("b_gcn", [P, 1])
        g_ln = sb("g_ln", [P, 1])
        b_ln = sb("b_ln", [P, 1])
        w_xz = sb("w_xz", [P, 2 * DI])
        w_cv = sb("w_cv", [P, CT, KC])
        b_cv = sb("b_cv", [P, CT])
        w_dbc = sb("w_dbc", [P, CT, P])
        w_dtp = sb("w_dtp", [P, DI])
        b_dtp = sb("b_dtp", [P, CT])
        neg_a = sb("neg_a", [P, CT, ST])
        d_sk = sb("d_sk", [P, CT])
        w_o = sb("w_o", [P, CT, D])
        carry = sb("carry", [P, CT * ST])
        conv_in = sb("conv_in", [P, CT, KC - 1 + CH])
        stats = sb("stats", [P, HT, 6])
        mv = sb("mv", [P, HT, 2])
        rstd = sb("rstd", [P, HT])
        nmr = sb("nmr", [P, HT])
        rinv = sb("rinv", [P, HT])
        rstd_s = sb("rstd_s", [P, HT])
        spare = sb("spare", [P, 5])
        low_sum = sb("low_sum", [P, HALVES * NT])
        low_row = sb("low_row", [P, 1])
        low_all = sb("low_all", [1, 1])

        ARENA = 29480
        arena = sb("arena", [P, ARENA])
        top1 = [0]
        top2 = [0]

        def carve(top, n):
            a = top[0]
            top[0] += n
            assert top[0] <= ARENA, top[0]
            return arena[:, a:a + n]

        def carve1(n):
            return carve(top1, n)

        def carve2(n):
            return carve(top2, n)

        masked = carve1(2 * HW).rearrange("p (b n) -> p b n", b=2)
        magnitude = carve1(2 * HW).rearrange("p (b n) -> p b n", b=2)
        abs_sum = carve1(HW)
        sup_t = carve1(HW).rearrange("p (k n) -> p k n", k=HC)
        y_left = carve1(NP // 2).bitcast(BF16)
        y_right = carve1(NP // 2).bitcast(BF16)
        h0r = carve1(NP).rearrange("p (n d) -> p n d", d=D)
        YW = CLS * NP // P
        y_full = carve1(YW)
        y_rest = carve1(YW)
        low_bits = carve1(HW // 2).bitcast(BF16)
        y_p = [carve1(YW // 2).bitcast(BF16) for _ in range(3)]

        def pair(a):
            return a.rearrange("p (b c n) -> p b c n", b=2, c=CT)

        def tiles(a):
            return a.rearrange("p (c n) -> p c n", c=CT)

        h_hi = carve2(NP // 2).bitcast(FP16).rearrange("p (n d) -> p n d", d=D)
        h_lo = carve2(NP // 2).bitcast(FP16).rearrange("p (n d) -> p n d", d=D)
        u = pair(carve2(2 * CT * CH))
        dt = pair(carve2(2 * CT * CH))
        dtu = tiles(carve2(CT * CH))
        z_gate = pair(carve2(2 * CT * CH))
        buf_a = carve2(CH)
        buf_b = carve2(CH)
        g_t = squares = normed = buf_a
        h_t = log_var = h_ln = buf_b
        centred = carve2(CH)
        z_t = tiles(carve2(CT * CH))
        dt_pos = tiles(carve2(CT * CH))
        conv_out = y_gated = tiles(carve2(CT * CH))
        dbc = carve2(CH)
        bc_rest = carve2(CH)
        bc_hi = carve2(CH // 2).bitcast(BF16)
        bc_mid = carve2(CH // 2).bitcast(BF16)
        dt_abs = z_t
        x_out = carve2(CH).rearrange("p (n d) -> p n d", d=D)
        decay = carve2(RING * CH).rearrange("p (b n) -> p b n", b=RING)
        drive = carve2(RING * CH).rearrange("p (b n) -> p b n", b=RING)
        state = carve2(RING * CH).rearrange("p (b n) -> p b n", b=RING)
        state_c = carve2(RING * CH).rearrange("p (b n) -> p b n", b=RING)
        b_row = carve2(2 * CH).rearrange("p (b n) -> p b n", b=2)
        bc3 = carve2(CH).bitcast(BF16).rearrange("p (b n) -> p b n", b=2)

        bank = ctx.enter_context(nc.psum_tensor("bank", [P, 8, CH], F32))
        G_BANK, M0, M1, B_BANK, C_BANK, Y_BANK = 0, 1, 2, 3, 4, 6

        x_loaded = [sem(f"x_loaded{i}") for i in range(NT // PIECE)]
        h0_loaded = sem("h0_loaded")
        y_loaded = sem("y_loaded")
        y_split = sem("y_split")
        y_stored = sem("y_stored")
        y_stacked = sem("y_stacked")
        w_loaded = sem("w_loaded")
        adj_loaded = [sem(f"adj_loaded{i}") for i in range(SLOTS)]
        const_set = sem("const_set")
        const_step = sem("const_step")
        zeroed = sem("zeroed")
        sel_ready = sem("sel_ready")
        neg_a_ready = sem("neg_a_ready")
        a_exp = sem("a_exp")
        stat_done = sem("stat_done")
        mv_done = sem("mv_done")
        lnv_small = sem("lnv_small")
        rstd_done = sem("rstd_done")
        nmr_done = sem("nmr_done")
        h0r_done = sem("h0r_done")
        x_mixed = sem("x_mixed")
        mask_done = sem("mask_done")
        prod_done = sem("prod_done")
        mag_done = sem("mag_done")
        abs_done = sem("abs_done")
        abs_pool_done = sem("abs_pool_done")
        sup_done = sem("sup_done")
        rows_done = sem("rows_done")
        abs_zeroed = sem("abs_zeroed")
        rinv_step = sem("rinv_step")
        sup_copied = sem("sup_copied")
        turned = sem("turned")
        x1_done = sem("x1_done")
        low_checked = sem("low_checked")
        low_added = sem("low_added")
        low_total = sem("low_total")
        low_known = sem("low_known")
        scaled_done = sem("scaled_done")
        h_hi_done = sem("h_hi_done")
        h_lo_done = sem("h_lo_done")
        paired_done = sem("paired_done")
        h1_done = sem("h1_done")

        g_done = sem("g_done")
        g_copied = sem("g_copied")
        gw_done = sem("gw_done")
        ht_done = sem("ht_done")
        mean_done = sem("mean_done")
        centred_done = sem("centred_done")
        sq_done = sem("sq_done")
        var_done = sem("var_done")
        lnv_done = sem("lnv_done")
        rs_done = sem("rs_done")
        normed_done = sem("normed_done")
        hln_done = sem("hln_done")
        xz_done = sem("xz_done")
        tail_done = sem("tail_done")
        cv_in_done = sem("cv_in_done")
        z_done = sem("z_done")
        zg_done = sem("zg_done")
        conv_step = sem("conv_step")
        u_done = sem("u_done")
        dbc_done = sem("dbc_done")
        dbc_copied = sem("dbc_copied")
        hi_done = sem("hi_done")
        bc3_hi = sem("bc3_hi")
        rest_done = sem("rest_done")
        mid_done = sem("mid_done")
        bc3_mid = sem("bc3_mid")
        bc3_lo = sem("bc3_lo")
        dtw_done = sem("dtw_done")
        dt_abs_done = sem("dt_abs_done")
        dt_pos_done = sem("dt_pos_done")
        dt_log_step = sem("dt_log_step")
        dt_done = sem("dt_done")
        dtu_done = sem("dtu_done")
        b_done = sem("b_done")
        c_done = sem("c_done")
        b_copied = sem("b_copied")
        decay_done = sem("decay_done")
        drive_done = sem("drive_done")
        scan_done = sem("scan_done")
        carried = sem("carried")
        sc_done = sem("sc_done")
        sum_done = sem("sum_done")
        y_mix = sem("y_mix")
        y_gate = sem("y_gate")
        o_done = sem("o_done")
        xo_done = sem("xo_done")
        stored = sem("stored")

        g_used = sem("g_used")
        CARRY0 = CT * ST
        SCAN0 = RING
        SUM0 = RING
        SC0 = 2
        DRIVE0 = 2
        STORED0 = 16

        block = ctx.enter_context(nc.Block())

        def over_chunks(eng, body):
            body(0, 0, False, True, True)
            pairs = (NC - 4) // 2
            with eng.Fori(0, pairs) as q:
                for i in range(2):
                    body(2 * q + 1 + i, (1 + i) % 2, True, True, True)
            for c in range(1 + 2 * pairs, NC):
                body(c, c % 2, True, c + 1 < NC, c + 2 < NC)

        def summed_before(c, i):
            if i < 0:
                n = -sum((j // CT) % ST + 1 not in PAIRED for j in range(CT * ST + i, CT * ST))
            else:
                n = sum(j // CT + 1 not in PAIRED for j in range(i))
            return c * (CT * (ST - len(PAIRED))) + n

        @block.sync
        def _(sp):
            x_v = x.rearrange("(n p) d -> p n d", p=P)
            h0_v = h0.rearrange("(n p) d -> p n d", p=P)
            y_v = y_t.rearrange("c (a m) -> (c a) m", m=YW)
            part_v = y_parts.rearrange("k c (a m) -> k (c a) m", m=YW)
            adj_rows = adj_t.rearrange("(j p) i -> j p i", p=P)
            adj_cols = adj_t.rearrange("(g j p) i -> g p j i", p=P, j=GJ)
            out_v = out[0:(NT - 1) * P, :].rearrange("(n p) d -> p n d", p=P)

            sp.dma_start(y_full, y_v).then_inc(y_loaded, 16)
            for i in range(NT // PIECE):
                sp.dma_start(x1[:, i * PIECE:(i + 1) * PIECE, :],
                             x_v[:, i * PIECE:(i + 1) * PIECE, :]).then_inc(x_loaded[i], 16)

            def load_rows(half, q):
                for r in range(SLOTS):
                    if not (half == 0 and isinstance(q, int) and q == 0):
                        sp.wait_ge(prod_done, HC * (half * NT + q * SLOTS + r - SLOTS + 1))
                        sp.wait_ge(low_checked, half * NT + q * SLOTS + r - SLOTS + 1)
                    sp.dma_start(adj_ring[:, r, :], adj_rows[q * SLOTS + r, :, half * HW:(half + 1) * HW]
                                 ).then_inc(adj_loaded[r], 16)

            load_rows(0, 0)
            sp.wait_ge(y_split, 5)
            for k in range(3):
                sp.dma_start(part_v[k], y_p[k]).then_inc(y_stored, 16)
            sp.wait_ge(y_stored, 3 * 16)
            for n, (a, b) in enumerate(Y_PAIRS):
                sp.dma_start(y_left[n * CLS:(n + 1) * CLS, :], y_parts[a]).then_inc(y_stacked, 16)
                sp.dma_start(y_right[n * CLS:(n + 1) * CLS, :], y_parts[b]).then_inc(y_stacked, 16)
            sp.dma_start(h1[:, :, :], h0_v).then_inc(h0_loaded, 16)
            for half in range(HALVES):
                with sp.Fori(1 if half == 0 else 0, NT // SLOTS) as q:
                    load_rows(half, q)

            def load_cols(k, groups=range(LPC)):
                for g in groups:
                    if isinstance(k, int) and k == 0 and g < SLOTS:
                        sp.wait_ge(prod_done, HC * (HALVES * NT - SLOTS + g + 1))
                        sp.wait_ge(low_checked, HALVES * NT - SLOTS + g + 1)
                    else:
                        sp.wait_ge(g_used, LPC * k + g - SLOTS + 1)
                    sp.dma_start(adj_ring[:, g % SLOTS, :].rearrange("p (j i) -> p j i", j=GJ),
                                 adj_cols[g, :, :, bass.ds(k * CH, CH)]).then_inc(adj_loaded[g % SLOTS], 16)

            def store(c):
                sp.wait_ge(xo_done, c + 1)
                sp.dma_start(out_v[:, bass.ds(c * TPC, TPC), :], x_out).then_inc(stored, 16)

            for k in range(3):
                load_cols(k)
            with sp.Fori(1, NC - 2) as c:
                load_cols(c + 2)
                store(c - 1)
            store(NC - 3)
            store(NC - 2)
            sp.wait_ge(xo_done, NC)
            sp.dma_start(out_v[:, (NC - 1) * TPC:NT - 1, :], x_out[:, 0:TPC - 1, :]).then_inc(stored, 16)
            sp.dma_start(out[(NT - 1) * P:N, :], x_out[0:LAST_ROWS, TPC - 1, :]).then_inc(stored, 16)
            sp.wait_ge(stored, STORED0 + (NC + 1) * 16)

        @block.gpsimd
        def _(pool):
            nc.gpsimd.memset(w_dbc[:], 0.0).then_inc(zeroed, 1)
            nc.gpsimd.memset(w_dtp[:], 0.0).then_inc(zeroed, 1)
            nc.gpsimd.memset(ident[:], 0.0).then_inc(const_step, 1)
            nc.gpsimd.memset(sel32[:], 0.0).then_inc(const_step, 1)
            nc.gpsimd.memset(mean_mat[:], 1.0 / D).then_inc(const_set, 1)
            nc.gpsimd.memset(ones[:], 1.0).then_inc(const_set, 1)
            nc.gpsimd.memset(ln_eps[:], LN_EPS).then_inc(const_set, 1)
            nc.gpsimd.memset(conv_in[:], 0.0).then_inc(const_set, 1)
            pool.wait_ge(const_step, 2)
            nc.gpsimd.affine_select(out=ident[:], in_=ident[:], compare_op=ALU.not_equal, fill=1.0, base=0,
                                    pattern=[[-1, P]], channel_multiplier=1).then_inc(const_set, 1)
            for q in range(1, 4):
                nc.gpsimd.affine_select(out=sel32[:], in_=sel32[:], compare_op=ALU.not_equal, fill=1.0,
                                        base=-2 * ST * q, pattern=[[-1, 2 * ST]],
                                        channel_multiplier=1).then_inc(const_step, 1)
                pool.wait_ge(const_step, 2 + q)
            nc.gpsimd.tensor_copy(sel[:], sel32[:]).then_inc(const_set, 1)
            nc.gpsimd.memset(carry[:], 0.0).then_inc(carried, CARRY0)
            nc.gpsimd.memset(spare[:, 0:1], 0.0).then_inc(scan_done, SCAN0)
            nc.gpsimd.memset(spare[:, 1:2], 0.0).then_inc(sum_done, SUM0)
            nc.gpsimd.memset(spare[:, 2:3], 0.0).then_inc(sc_done, SC0)
            nc.gpsimd.memset(spare[:, 3:4], 0.0).then_inc(drive_done, DRIVE0)
            nc.gpsimd.memset(spare[:, 4:5], 0.0).then_inc(stored, STORED0)

            def add_magnitudes(half, q):
                for r in range(SLOTS):
                    tile = half * NT + q * SLOTS + r
                    pool.wait_ge(mag_done, tile + 1)
                    pool.wait_ge(abs_pool_done, tile + half + 1)
                    nc.gpsimd.tensor_tensor(abs_sum[:, VW:HW], magnitude[:, r % 2, VW:HW], abs_sum[:, VW:HW],
                                            ALU.add).then_inc(abs_pool_done, 1)

            for half in range(HALVES):
                if half > 0:
                    pool.wait_ge(rows_done, half)
                nc.gpsimd.memset(abs_sum[:, VW:HW], 0.0).then_inc(abs_pool_done, 1)
                with pool.Fori(0, NT // SLOTS) as q:
                    add_magnitudes(half, q)

            def pre(step, k, pb):
                if step == 11:
                    pool.wait_ge(hi_done, k + 1)
                    pool.wait_ge(dbc_copied, k + 1)
                    nc.gpsimd.tensor_tensor(bc_rest, dbc, bc_hi, ALU.subtract).then_inc(rest_done, 1)
                if step == 12:
                    pool.wait_ge(mid_done, k + 1)
                    if not (isinstance(k, int) and k == 0):
                        pool.wait_ge(carried, CARRY0 + CT * ST * (k - 1) + CT * step)
                    nc.gpsimd.tensor_tensor(bc3[96:128, pb, :], bc_rest[96:128, :], bc_mid[96:128, :],
                                            ALU.subtract).then_inc(bc3_lo, 1)
                    pool.wait_ge(bc3_lo, k + 1)

            def dt_times_u(k, pb):
                pool.wait_ge(dt_done, k + 1)
                pool.wait_ge(u_done, k + 1)
                nc.gpsimd.tensor_tensor(dtu, dt[:, pb], u[:, pb], ALU.mult).then_inc(dtu_done, 1)

            def carry_over(v, i):
                pool.wait_ge(scan_done, SCAN0 + v + 1)
                nc.gpsimd.tensor_tensor(carry[:, i:i + 1], state[:, i % RING, CH - 1:CH], ones[:],
                                        ALU.mult).then_inc(carried, 1)

            def body(c, b, do_tail, do_pre, do_gcn):
                pool.wait_ge(dtu_done, c + 1)
                for s in range(ST):
                    for ct in range(CT):
                        i = s * CT + ct
                        v = c * (CT * ST) + i
                        if ct == 0:
                            pool.wait_ge(b_copied, c * ST + s + 1)
                        pool.wait_ge(scan_done, SCAN0 + v - RING + 1)
                        nc.gpsimd.tensor_tensor(drive[:, i % RING, :], dtu[:, ct, :], b_row[:, s % 2, :],
                                                ALU.mult).then_inc(drive_done, 1)
                        if i >= 2:
                            carry_over(v - 2, i - 2)
                    if do_pre:
                        pre(s, c + 1, 1 - b)
                for i in range(CT * ST - 2, CT * ST):
                    carry_over(c * (CT * ST) + i, i)
                if do_pre:
                    dt_times_u(c + 1, 1 - b)

            for s in range(ST):
                pre(s, 0, 0)
            dt_times_u(0, 0)
            over_chunks(pool, body)

        @block.tensor
        def _(pe):
            pe.wait_ge(const_set, 6)
            pe.wait_ge(y_stacked, 2 * len(Y_PAIRS) * 16)

            UNITS = NT * HC
            with pe.Fori(0, HALVES) as half:
                def mask(m):
                    j, k = divmod(m, HC)
                    if m >= 2:
                        pe.wait_ge(prod_done, half * UNITS + m - 1)
                    nc.tensor.matmul(bank[:, 6 + m % 2, :], y_left[:, j * P:(j + 1) * P],
                                     y_right[:, bass.ds(half * HW + k * CH, CH)],
                                     start=True, stop=True).then_inc(mask_done, 1)

                mask(0)
                for m in range(UNITS):
                    j, k = divmod(m, HC)
                    if m + 1 < UNITS:
                        mask(m + 1)
                    if k == 0:
                        pe.wait_ge(h0r_done, j + 1)
                    pe.wait_ge(prod_done, half * UNITS + m + 1)
                    nc.tensor.matmul(bank[:, k, :], h0r[:, j, :], masked[:, j % 2, k * CH:(k + 1) * CH],
                                     start=(j == 0), stop=(j == NT - 1)).then_inc(sup_done, 1)
                pe.wait_ge(abs_done, half * NT + NT)
                pe.wait_ge(abs_pool_done, (half + 1) * (NT + 1))
                for i in range(HT):
                    last = nc.tensor.matmul(bank[:, 5, i:i + 1], abs_sum[:, i * P:(i + 1) * P], ones[:],
                                            start=True, stop=True)
                last.then_inc(rows_done, 1)
                for k in range(HC):
                    pe.wait_ge(sup_copied, half * HC + k + 1)
                    if k >= 2:
                        pe.wait_ge(x1_done, half * HT + TPC * (k - 1))
                    for i in range(TPC):
                        last = nc.tensor.transpose(bank[:, 6 + k % 2, i * P:(i + 1) * P],
                                                   sup_t[:, k, i * P:(i + 1) * P], ident[:])
                    last.then_inc(turned, 1)
                pe.wait_ge(x1_done, (half + 1) * HT)

            pe.wait_ge(low_added, 1)
            nc.tensor.matmul(bank[0:1, 5, 0:1], low_row[:], ones[:], start=True, stop=True).then_inc(low_total, 1)
            pe.wait_ge(low_known, 1)
            low_bits_sum = pe.value_load(low_all[:].bitcast(I32))

            def k_is_first(k):
                return isinstance(k, int) and k == 0

            def graph(k, tiles_, exact):
                for j in tiles_:
                    g, r = divmod(j, GJ)
                    if j == 0:
                        pe.wait_ge(g_copied, k)
                    if r == 0:
                        pe.wait_ge(adj_loaded[g % SLOTS],
                                   16 * (HALVES * NT // SLOTS + (LPC // SLOTS) * k + g // SLOTS + 1))
                    part = adj_ring[:, g % SLOTS, r * CH:(r + 1) * CH]
                    if exact:
                        if k_is_first(k) and j % PIECE == 0:
                            pe.wait_ge(h_lo_done, j // PIECE + 1)
                        high = part.bitcast(BF16).rearrange("p (n two) -> p n two", two=2)[:, :, 1]
                        nc.tensor.matmul(bank[:, G_BANK, :], h_hi[:, j, :], high, start=(j == 0), stop=False)
                        mm = nc.tensor.matmul(bank[:, G_BANK, :], h_lo[:, j, :], high, start=False,
                                              stop=(j == NT - 1))
                    else:
                        mm = nc.tensor.matmul(bank[:, G_BANK, :], h1[:, j, :], part,
                                              start=(j == 0), stop=(j == NT - 1))
                    if r == GJ - 1:
                        mm.then_inc(g_used, 1)

            def pre(step, k, pb):
                if step == 1:
                    pe.wait_ge(g_copied, k + 1)
                    pe.wait_ge(dt_abs_done, CT * k)
                    pe.wait_ge(dt_pos_done, CT * k)
                    nc.tensor.matmul(bank[:, M0, :], w_gcn[:], g_t, start=True, stop=True).then_inc(gw_done, 1)
                if step == 2:
                    pe.wait_ge(ht_done, k + 1)
                    nc.tensor.matmul(bank[:, M1, :], mean_mat[:], h_t, start=True, stop=True).then_inc(mean_done, 1)
                if step == 5:
                    pe.wait_ge(sq_done, k + 1)
                    nc.tensor.matmul(bank[:, M0, :], mean_mat[:], squares, start=True, stop=True).then_inc(var_done, 1)
                if step == 7:
                    pe.wait_ge(hln_done, k + 1)
                    if not k_is_first(k):
                        pe.wait_ge(xo_done, k - 1)
                    for m in range(2):
                        nc.tensor.matmul(bank[:, M0 + m, :], w_xz[:, m * P:(m + 1) * P], h_ln,
                                         start=True, stop=True).then_inc(xz_done, 1)
                if step == 8:
                    for m in range(2):
                        pe.wait_ge(cv_in_done, CT * k + m + 1)
                        nc.tensor.matmul(bank[:, M0 + m, :], w_xz[:, DI + m * P:DI + (m + 1) * P], h_ln,
                                         start=True, stop=True).then_inc(xz_done, 1)
                if step == 11:
                    pe.wait_ge(u_done, k + 1)
                    pe.wait_ge(z_done, CT * k + 1)
                    for t in range(CT):
                        mm = nc.tensor.matmul(bank[:, M0, :], w_dbc[:, t, :], u[:, pb, t, :],
                                              start=(t == 0), stop=(t == CT - 1))
                    mm.then_inc(dbc_done, 1)
                if step == 12:
                    pe.wait_ge(dbc_copied, k + 1)
                    pe.wait_ge(z_done, CT * k + 2)
                    nc.tensor.matmul(bank[:, M1, :], w_dtp[:, 0:P], dbc, start=True, stop=True).then_inc(dtw_done, 1)
                    pe.wait_ge(bc3_hi, k + 1)
                    nc.tensor.matmul(bank[:, M0, :], w_dtp[:, P:DI], dbc, start=True, stop=True).then_inc(dtw_done, 1)

            def second_layer(exact):
                def sums(c, s):
                    for t in range(CT):
                        i = s * CT + t
                        v = c * (CT * ST) + i
                        if s + 1 in PAIRED:
                            continue
                        if i == 0:
                            pe.wait_ge(y_mix, CT * c)
                        if s in PAIRED:
                            pe.wait_ge(paired_done, c * (CT * len(PAIRED)) + PAIRED.index(s) * CT + t + 1)
                        else:
                            pe.wait_ge(sc_done, SC0 + v + 1)
                        nc.tensor.matmul(bank[:, Y_BANK + t, :], ident[:], state_c[:, i % RING, :],
                                         start=(s == 0), stop=(s == ST - 1)).then_inc(sum_done, 1)

                def spread_b(c, b, s):
                    n = c * ST + s
                    if s == 0:
                        pe.wait_ge(bc3_hi, c + 1)
                        pe.wait_ge(bc3_mid, c + 1)
                        pe.wait_ge(bc3_lo, c + 1)
                    pe.wait_ge(b_copied, n)
                    nc.tensor.matmul(bank[:, B_BANK, :], sel[:, s:s + 1].to_broadcast([P, P]), bc3[:, b, :],
                                     start=True, stop=True).then_inc(b_done, 1)

                def spread_c(c, b, s):
                    pe.wait_ge(sc_done, SC0 + CT * (c * ST + s - 1))
                    nc.tensor.matmul(bank[:, C_BANK + s % 2, :], sel[:, ST + s:ST + s + 1].to_broadcast([P, P]),
                                     bc3[:, b, :], start=True, stop=True).then_inc(c_done, 1)

                def project(c, prepared):
                    pe.wait_ge(y_gate, c + 1)
                    if prepared:
                        pe.wait_ge(centred_done, c + 3)
                    else:
                        pe.wait_ge(dt_abs_done, CT * NC)
                    for i in range(TPC):
                        for t in range(CT):
                            mm = nc.tensor.matmul(bank[:, M1, i * P:(i + 1) * P], y_gated[:, t, i * P:(i + 1) * P],
                                                  w_o[:, t, :], start=(t == 0), stop=(t == CT - 1))
                    mm.then_inc(o_done, 1)

                def body(c, b, do_tail, do_pre, do_gcn):
                    for s in range(ST):
                        if s + 1 < ST:
                            spread_b(c, b, s + 1)
                        elif do_pre:
                            spread_b(c + 1, 1 - b, 0)
                        if do_gcn and s > 0:
                            graph(c + 2, range(NT * (s - 1) // (ST - 1), NT * s // (ST - 1)), exact)
                        if do_pre:
                            pre(s, c + 1, 1 - b)
                        if s >= 2:
                            sums(c, s - 2)
                        elif do_tail:
                            sums(c - 1, ST - 2 + s)
                        if do_tail and s == OUT_STEP:
                            project(c - 1, do_pre)
                        if s + 1 < ST:
                            spread_c(c, b, s + 1)
                        elif do_pre:
                            spread_c(c + 1, 1 - b, 0)

                graph(0, range(NT), exact)
                pe.wait_ge(g_copied, 1)
                per_step = NT // ST + 1
                for s in range(ST):
                    graph(1, range(min(NT, s * per_step), min(NT, (s + 1) * per_step)), exact)
                    pre(s, 0, 0)
                spread_b(0, 0, 0)
                spread_c(0, 0, 0)
                over_chunks(pe, body)
                sums(NC - 1, ST - 2)
                sums(NC - 1, ST - 1)
                project(NC - 1, False)

            pe.wait_ge(h1_done, NT)
            pe.wait_ge(w_loaded, N_WEIGHTS * 16)
            with pe.If(low_bits_sum == 0):
                second_layer(True)
            with pe.Else():
                second_layer(False)

        @block.scalar
        def _(act):
            act.preload_act_table_set("natural_log_exp_and_others")
            act.wait_ge(zeroed, 2)
            xp_v = w_xp.rearrange("(t p) n -> p t n", p=P)
            loads = [(w_dbc[:, :, 0:RK], xp_v[:, :, 0:RK])]
            loads += [(w_dbc[:, :, 2 * ST * q:2 * ST * (q + 1)], xp_v[:, :, RK:RK + 2 * ST]) for q in range(1, 4)]
            loads += [(w_dtp[0:RK, :], w_dt), (w_gcn[:], gcn_w), (b_gcn[:], gcn_b), (g_ln[:], ln_g), (b_ln[:], ln_b),
                      (w_xz[:], w_in), (w_cv[:], conv_w.rearrange("(t p) k -> p t k", p=P)),
                      (b_cv[:], conv_b), (b_dtp[:], b_dt), (d_sk[:], d_skip),
                      (neg_a[:], a_log.rearrange("(t p) s -> p t s", p=P)),
                      (w_o[:], w_out.rearrange("(t p) n -> p t n", p=P))]
            assert len(loads) == N_WEIGHTS
            for dst, src in loads:
                act.dma_start(dst, src).then_inc(w_loaded, 16)
            act.wait_ge(const_set, 3)

            def norm_group(g, src, dst, n, first, at, done, scale=rstd):
                act.wait_ge(mv_done, g + 1)
                act.activation(rstd[:, at:at + n], mv[:, at:at + n, 1], ACT.Ln, bias=ln_eps[:]).then_inc(lnv_small, 1)
                act.wait_ge(lnv_small, g + 1)
                act.activation(rstd[:, at:at + n], rstd[:, at:at + n], ACT.Exp, scale=-0.5).then_inc(rstd_done, 1)
                act.wait_ge(nmr_done, g + 1)
                for i in range(n):
                    act.activation(dst[:, first + i, :], src[:, first + i, :], ACT.Relu,
                                   bias=nmr[:, at + i:at + i + 1], scale=scale[:, at + i:at + i + 1]).then_inc(done, 1)

            for g in range(NT // PIECE):
                norm_group(g, x1, h0r, PIECE, g * PIECE, PIECE * (g % 2), h0r_done)
            def magnitudes(half, q):
                for r in range(SLOTS):
                    tile = half * NT + q * SLOTS + r
                    act.wait_ge(adj_loaded[r], 16 * (half * (NT // SLOTS) + q + 1))
                    act.wait_ge(low_checked, tile)
                    act.activation(low_bits, adj_ring[:, r, :].bitcast(U16).rearrange("p (n two) -> p n two", two=2)[:, :, 0],
                                   ACT.Copy, accum_out=low_sum[:, bass.ds(tile, 1)]).then_inc(low_checked, 1)
                    act.wait_ge(prod_done, HC * (tile + 1))
                    if not (isinstance(q, int) and half == 0 and r < 2):
                        act.wait_ge(abs_done, tile - 1)
                        act.wait_ge(abs_pool_done, tile + half)
                    act.activation(magnitude[:, r % 2, :], masked[:, r % 2, :], ACT.Abs).then_inc(mag_done, 1)

            for half in range(HALVES):
                magnitudes(half, 0)
                with act.Fori(1, NT // SLOTS) as q:
                    magnitudes(half, q)
                for k in range(HC):
                    act.wait_ge(sup_done, (half + 1) * NT * HC - HC + k + 1)
                    if k == 0 and half > 0:
                        act.wait_ge(turned, half * HC)
                    act.activation(sup_t[:, k, :], bank[:, k, :], ACT.Copy).then_inc(sup_copied, 1)
                norm_group(NT // PIECE + half, x1, h1, HT, half * HT, 0, h1_done, rstd_s)

            act.wait_ge(h1_done, NT)
            act.wait_ge(sup_done, HALVES * NT * HC)
            for i in range(NT // PIECE):
                act.activation(h_hi[:, i * PIECE:(i + 1) * PIECE, :], h1[:, i * PIECE:(i + 1) * PIECE, :],
                               ACT.Copy).then_inc(h_hi_done, 1)

            act.wait_ge(w_loaded, N_WEIGHTS * 16)
            act.activation(neg_a[:], neg_a[:], ACT.Exp).then_inc(a_exp, 1)
            act.wait_ge(a_exp, 1)
            act.activation(neg_a[:], neg_a[:], ACT.Copy, scale=-1.0).then_inc(neg_a_ready, 1)
            act.wait_ge(neg_a_ready, 1)

            def pre(step, k, pb):
                if step == 0:
                    act.wait_ge(g_used, LPC * (k + 1))
                    act.activation(g_t, bank[:, G_BANK, :], ACT.Copy, scale=1.0 / H_SCALE).then_inc(g_copied, 1)
                if step == 1:
                    act.wait_ge(gw_done, k + 1)
                    act.activation(h_t, bank[:, M0, :], ACT.Relu, bias=b_gcn[:]).then_inc(ht_done, 1)
                if step == 4:
                    act.wait_ge(centred_done, k + 1)
                    act.activation(squares, centred, ACT.Square).then_inc(sq_done, 1)
                if step == 5:
                    act.wait_ge(var_done, k + 1)
                    act.activation(log_var, bank[:, M0, :], ACT.Ln, bias=ln_eps[:]).then_inc(lnv_done, 1)
                    act.wait_ge(lnv_done, k + 1)
                    act.activation(log_var, log_var, ACT.Exp, scale=-0.5).then_inc(rs_done, 1)
                if step == 7:
                    act.wait_ge(normed_done, k + 1)
                    act.activation(h_ln, normed, ACT.Identity, bias=b_ln[:]).then_inc(hln_done, 1)
                if step == 7:
                    act.wait_ge(conv_step, CT * KC * k)
                    act.activation(conv_in[:, :, 0:KC - 1], conv_in[:, :, CH:CH + KC - 1], ACT.Copy).then_inc(tail_done, 1)
                    act.wait_ge(tail_done, k + 1)
                    for t in range(CT):
                        act.wait_ge(xz_done, 2 * CT * k + t + 1)
                        act.activation(conv_in[:, t, KC - 1:], bank[:, M0 + t, :], ACT.Copy).then_inc(cv_in_done, 1)
                if step == 8:
                    for t in range(CT):
                        act.wait_ge(xz_done, 2 * CT * k + CT + t + 1)
                        act.activation(z_t[:, t, :], bank[:, M0 + t, :], ACT.Copy).then_inc(z_done, 1)
                if step == 10:
                    act.preload_act_table_set("silu_and_others")
                    if not (isinstance(k, int) and k == 0):
                        act.wait_ge(y_gate, k - 1)
                    act.wait_ge(z_done, CT * (k + 1))
                    act.activation(z_gate[:, pb], z_t, ACT.Silu).then_inc(zg_done, 1)
                    act.wait_ge(conv_step, CT * KC * (k + 1))
                    act.activation(u[:, pb], conv_out, ACT.Silu).then_inc(u_done, 1)
                    act.preload_act_table_set("natural_log_exp_and_others")
                if step == 11:
                    act.wait_ge(dbc_done, k + 1)
                    act.activation(bc_hi, bank[:, M0, :], ACT.Copy).then_inc(hi_done, 1)
                    act.activation(dbc, bank[:, M0, :], ACT.Copy).then_inc(dbc_copied, 1)
                    act.activation(bc3[0:64, pb, :], bank[0:64, M0, :], ACT.Copy).then_inc(bc3_hi, 1)
                if step == 12:
                    act.wait_ge(rest_done, k + 1)
                    act.activation(bc_mid, bc_rest, ACT.Copy).then_inc(mid_done, 1)
                    act.activation(bc3[64:96, pb, :], bc_rest[64:96, :], ACT.Copy).then_inc(bc3_mid, 1)
                if step == 13:
                    act.wait_ge(zg_done, k + 1)
                    for t in range(CT):
                        act.wait_ge(dtw_done, CT * k + t + 1)
                        act.activation(dt_pos[:, t, :], bank[:, M1 - t, :], ACT.Relu,
                                       bias=b_dtp[:, t:t + 1]).then_inc(dt_pos_done, 1)
                        act.activation(dt_abs[:, t, :], bank[:, M1 - t, :], ACT.Abs,
                                       bias=b_dtp[:, t:t + 1]).then_inc(dt_abs_done, 1)
                    act.wait_ge(dt_abs_done, CT * (k + 1))
                    act.activation(dt_abs, dt_abs, ACT.Exp, scale=-1.0).then_inc(dt_log_step, 1)
                    act.wait_ge(dt_log_step, 2 * k + 1)
                    act.activation(dt_abs, dt_abs, ACT.Ln, bias=ones[:]).then_inc(dt_log_step, 1)

            def body(c, b, do_tail, do_pre, do_gcn):
                act.wait_ge(dt_done, c + 1)
                for s in range(ST):
                    n = c * ST + s
                    act.wait_ge(b_done, n + 1)
                    act.wait_ge(drive_done, DRIVE0 + CT * (n - 1))
                    act.activation(b_row[:, s % 2, :], bank[:, B_BANK, :], ACT.Copy).then_inc(b_copied, 1)
                    for t in range(CT):
                        i = s * CT + t
                        v = c * (CT * ST) + i
                        act.wait_ge(scan_done, SCAN0 + v - RING + 1)
                        act.activation(decay[:, i % RING, :], dt[:, b, t, :], ACT.Exp,
                                       scale=neg_a[:, t, s:s + 1]).then_inc(decay_done, 1)
                    if do_pre:
                        pre(s, c + 1, 1 - b)

            for s in range(ST):
                pre(s, 0, 0)
            over_chunks(act, body)

        @block.vector
        def _(dve):
            dve.wait_ge(y_loaded, 16)
            nc.vector.tensor_copy(y_p[0], y_full).then_inc(y_split, 1)
            dve.wait_ge(y_split, 1)
            nc.vector.tensor_tensor(y_rest, y_full, y_p[0], ALU.subtract).then_inc(y_split, 1)
            dve.wait_ge(y_split, 2)
            nc.vector.tensor_copy(y_p[1], y_rest).then_inc(y_split, 1)
            dve.wait_ge(y_split, 3)
            nc.vector.tensor_tensor(y_rest, y_rest, y_p[1], ALU.subtract).then_inc(y_split, 1)
            dve.wait_ge(y_split, 4)
            nc.vector.tensor_copy(y_p[2], y_rest).then_inc(y_split, 1)

            def stat_group(g, src, n, first, at, base):
                for i in range(n):
                    nc.vector.bn_stats(stats[:, at + i, :], src[:, first + i, :]).then_inc(stat_done, 1)
                for i in range(n):
                    dve.wait_ge(stat_done, base + i + 1)
                    agg = nc.vector.bn_aggr(mv[:, at + i, :], stats[:, at + i, :])
                agg.then_inc(mv_done, 1)

            def nmr_group(g, n, at, scale=rstd):
                dve.wait_ge(rstd_done, g + 1)
                if scale is rstd_s:
                    nc.vector.tensor_scalar(rstd_s[:, at:at + n], rstd[:, at:at + n], H_SCALE, None,
                                            ALU.mult).then_inc(scaled_done, 1)
                    dve.wait_ge(scaled_done, g - NT // PIECE + 1)
                nc.vector.scalar_tensor_tensor(nmr[:, at:at + n], mv[:, at:at + n, 0], -1.0, scale[:, at:at + n],
                                               ALU.mult, ALU.mult).then_inc(nmr_done, 1)

            for g in range(NT // PIECE):
                dve.wait_ge(x_loaded[g], 16)
                stat_group(g, x1, PIECE, g * PIECE, PIECE * (g % 2), g * PIECE)
                nmr_group(g, PIECE, PIECE * (g % 2))
            dve.wait_ge(h0_loaded, 16)
            dve.wait_ge(h0r_done, NT)
            nc.vector.scalar_tensor_tensor(x1.rearrange("p n d -> p (n d)"), h1.rearrange("p n d -> p (n d)"), ALPHA,
                                           x1.rearrange("p n d -> p (n d)"), ALU.mult, ALU.add).then_inc(x_mixed, 1)

            def mask_group(half, q, first):
                for r in range(SLOTS):
                    tile = half * NT + q * SLOTS + r
                    dve.wait_ge(adj_loaded[r], 16 * (half * (NT // SLOTS) + q + 1))
                    if not (first and r < 2):
                        dve.wait_ge(sup_done, HC * (tile - 1))
                        dve.wait_ge(mag_done, tile - 1)
                    for k in range(HC):
                        dve.wait_ge(mask_done, HC * tile + k + 1)
                        nc.vector.tensor_tensor(masked[:, r % 2, k * CH:(k + 1) * CH], bank[:, 6 + (r + k) % 2, :],
                                                adj_ring[:, r, k * CH:(k + 1) * CH], ALU.mult).then_inc(prod_done, 1)
                    if not (first and r == 0):
                        add_magnitudes(tile - 1, (r - 1) % 2)

            def add_magnitudes(tile, slot):
                dve.wait_ge(mag_done, tile + 1)
                dve.wait_ge(abs_done, tile)
                nc.vector.tensor_tensor(abs_sum[:, 0:VW], magnitude[:, slot, 0:VW], abs_sum[:, 0:VW],
                                        ALU.add).then_inc(abs_done, 1)

            for half in range(HALVES):
                if half > 0:
                    dve.wait_ge(rows_done, half)
                nc.vector.memset(abs_sum[:, 0:VW], 0.0).then_inc(abs_zeroed, 1)
                dve.wait_ge(abs_zeroed, half + 1)
                mask_group(half, 0, True)
                with dve.Fori(1, NT // SLOTS) as q:
                    mask_group(half, q, False)
                add_magnitudes(half * NT + NT - 1, 1)
                dve.wait_ge(rows_done, half + 1)
                nc.vector.tensor_scalar(rinv[:], bank[:, 5, 0:HT], ROW_EPS, None, ALU.max).then_inc(rinv_step, 1)
                dve.wait_ge(rinv_step, 3 * half + 1)
                nc.vector.reciprocal(rinv[:], rinv[:]).then_inc(rinv_step, 1)
                dve.wait_ge(rinv_step, 3 * half + 2)
                nc.vector.tensor_scalar(rinv[:], rinv[:], 1.0 - ALPHA, None, ALU.mult).then_inc(rinv_step, 1)
                dve.wait_ge(rinv_step, 3 * half + 3)
                dve.wait_ge(x_mixed, 1)
                for k in range(HC):
                    dve.wait_ge(turned, half * HC + k + 1)
                    for i in range(TPC):
                        n = k * TPC + i
                        nc.vector.scalar_tensor_tensor(x1[:, half * HT + n, :], bank[:, 6 + k % 2, i * P:(i + 1) * P],
                                                       rinv[:, n:n + 1], x1[:, half * HT + n, :],
                                                       ALU.mult, ALU.add).then_inc(x1_done, 1)
                dve.wait_ge(x1_done, (half + 1) * HT)
                stat_group(NT // PIECE + half, x1, HT, half * HT, 0, NT + half * HT)
                nmr_group(NT // PIECE + half, HT, 0, rstd_s)

            dve.wait_ge(low_checked, HALVES * NT)
            nc.vector.reduce_sum(low_row[:], low_sum[:], axis=mybir.AxisListType.X).then_inc(low_added, 1)
            dve.wait_ge(low_total, 1)
            nc.vector.tensor_copy(low_all[:], bank[0:1, 5, 0:1]).then_inc(low_known, 1)
            for i in range(NT // PIECE):
                dve.wait_ge(h_hi_done, i + 1)
                nc.vector.tensor_tensor(h_lo[:, i * PIECE:(i + 1) * PIECE, :], h1[:, i * PIECE:(i + 1) * PIECE, :],
                                        h_hi[:, i * PIECE:(i + 1) * PIECE, :], ALU.subtract).then_inc(h_lo_done, 1)

            def pre(step, k, pb):
                if step == 2:
                    dve.wait_ge(mean_done, k + 1)
                    nc.vector.tensor_tensor(centred, h_t, bank[:, M1, :], ALU.subtract).then_inc(centred_done, 1)
                if step == 5:
                    dve.wait_ge(rs_done, k + 1)
                    nc.vector.scalar_tensor_tensor(normed, centred, g_ln[:], log_var, ALU.mult,
                                                   ALU.mult).then_inc(normed_done, 1)
                if step in (7, 8):
                    t = step - 7
                    dve.wait_ge(cv_in_done, CT * k + t + 1)
                    if t == 0:
                        dve.wait_ge(u_done, k)
                        if not (isinstance(k, int) and k == 0):
                            dve.wait_ge(o_done, k - 1)
                    base = CT * KC * k + KC * t
                    nc.vector.tensor_scalar(conv_out[:, t, :], conv_in[:, t, 0:CH], w_cv[:, t, 0:1], b_cv[:, t:t + 1],
                                            ALU.mult, ALU.add).then_inc(conv_step, 1)
                    for j in range(1, KC):
                        dve.wait_ge(conv_step, base + j)
                        nc.vector.scalar_tensor_tensor(conv_out[:, t, :], conv_in[:, t, j:j + CH], w_cv[:, t, j:j + 1],
                                                       conv_out[:, t, :], ALU.mult, ALU.add).then_inc(conv_step, 1)
                if step == 13:
                    dve.wait_ge(dt_log_step, 2 * (k + 1))
                    dve.wait_ge(dt_pos_done, CT * (k + 1))
                    nc.vector.tensor_tensor(dt[:, pb], dt_pos, dt_abs, ALU.add).then_inc(dt_done, 1)

            def tail(step, c, b):
                if step == 1:
                    if isinstance(c, int) and c == NC - 1:
                        dve.wait_ge(u_done, NC)
                        dve.wait_ge(o_done, NC - 1)
                    else:
                        dve.wait_ge(u_done, c + 2)
                    for t in range(CT):
                        dve.wait_ge(sum_done, SUM0 + summed_before(c, CT * ST) - CT + t + 1)
                        nc.vector.scalar_tensor_tensor(y_gated[:, t, :], u[:, b, t, :], d_sk[:, t:t + 1],
                                                       bank[:, Y_BANK + t, :], ALU.mult, ALU.add).then_inc(y_mix, 1)
                if step == 2:
                    dve.wait_ge(y_mix, CT * (c + 1))
                    nc.vector.tensor_tensor(y_gated, y_gated, z_gate[:, b], ALU.mult).then_inc(y_gate, 1)
                if step == OUT_STEP:
                    dve.wait_ge(o_done, c + 1)
                    dve.wait_ge(stored, STORED0 + 16 * c)
                    nc.vector.tensor_tensor(x_out, bank[:, M1, :].rearrange("p (n d) -> p n d", d=D),
                                            x1[:, bass.ds(c * TPC, TPC), :], ALU.add).then_inc(xo_done, 1)

            def body(c, b, do_tail, do_pre, do_gcn):
                def times_c(i):
                    v = c * (CT * ST) + i
                    dve.wait_ge(c_done, c * ST + i // CT + 1)
                    dve.wait_ge(scan_done, SCAN0 + v + 1)
                    dve.wait_ge(sum_done, SUM0 + summed_before(c, i - RING + 1))
                    nc.vector.tensor_tensor(state_c[:, i % RING, :], state[:, i % RING, :],
                                            bank[:, C_BANK + (i // CT) % 2, :], ALU.mult).then_inc(sc_done, 1)
                    if i // CT in PAIRED:
                        dve.wait_ge(sc_done, SC0 + v + 1)
                        nc.vector.tensor_tensor(state_c[:, i % RING, :], state_c[:, i % RING, :],
                                                state_c[:, (i - CT) % RING, :], ALU.add).then_inc(paired_done, 1)

                for s in range(ST):
                    for t in range(CT):
                        i = s * CT + t
                        v = c * (CT * ST) + i
                        dve.wait_ge(decay_done, v + 1)
                        dve.wait_ge(drive_done, DRIVE0 + v + 1)
                        dve.wait_ge(carried, CARRY0 + v - RING + 1)
                        nc.vector.tensor_tensor_scan(state[:, i % RING, :], decay[:, i % RING, :],
                                                     drive[:, i % RING, :], carry[:, i:i + 1],
                                                     ALU.mult, ALU.add).then_inc(scan_done, 1)
                        if i > 0:
                            times_c(i - 1)
                    if do_tail:
                        tail(s, c - 1, 1 - b)
                    if do_pre:
                        pre(s, c + 1, 1 - b)
                times_c(CT * ST - 1)

            for s in range(ST):
                pre(s, 0, 0)
            over_chunks(dve, body)
            for s in range(ST):
                tail(s, NC - 1, (NC - 1) % 2)


def kernel(x, adj, L0_gnn_h0, L0_gnn_y, L1_gnn_gcn_w, L1_gnn_gcn_b, L1_gnn_ln_g, L1_gnn_ln_b, L1_gnn_w_in,
           L1_gnn_conv_w, L1_gnn_conv_b, L1_gnn_w_xp, L1_gnn_w_dt, L1_gnn_b_dt, L1_gnn_A_log, L1_gnn_D_skip,
           L1_gnn_w_out):
    import numpy as np
    import concourse.bacc as bacc
    from concourse.bass_utils import run_bass_kernel_spmd

    def rows(a):
        a = np.asarray(a)
        return np.concatenate([a, np.zeros((NP - N,) + a.shape[1:], a.dtype)])

    def columns(a):
        return np.ascontiguousarray(np.asarray(a).reshape(-1, P).T)

    adj_t = np.zeros((NP, NP), np.asarray(adj).dtype)
    adj_t[:N, :N] = np.asarray(adj).T
    y_t = np.ascontiguousarray(rows(L0_gnn_y).T)
    arrays = [("x", rows(x)), ("h0", rows(L0_gnn_h0)), ("adj_t", adj_t), ("y_t", y_t),
              ("gcn_w", L1_gnn_gcn_w), ("gcn_b", columns(L1_gnn_gcn_b)), ("ln_g", columns(L1_gnn_ln_g)),
              ("ln_b", columns(L1_gnn_ln_b)), ("w_in", L1_gnn_w_in), ("conv_w", L1_gnn_conv_w),
              ("conv_b", columns(L1_gnn_conv_b)), ("w_xp", L1_gnn_w_xp), ("w_dt", L1_gnn_w_dt),
              ("b_dt", columns(L1_gnn_b_dt)), ("a_log", L1_gnn_A_log), ("d_skip", columns(L1_gnn_D_skip)),
              ("w_out", L1_gnn_w_out)]
    nc = bacc.Bacc("TRN2", target_bir_lowering=False, num_devices=1)
    feed, args = {}, []
    for name, a in arrays:
        a = np.ascontiguousarray(a)
        feed[f"in_{name}"] = a
        args.append(nc.dram_tensor(f"in_{name}", a.shape, mybir.dt.from_np(a.dtype), kind="ExternalInput").ap())
    out = nc.dram_tensor("out_x", (N, D), F32, kind="ExternalOutput").ap()
    build(nc, *args, out)
    r = run_bass_kernel_spmd(nc, [feed], core_ids=[0])
    return r.results[0]["out_x"]
```

```python
import concourse.bass as bass
from concourse import mybir
from contextlib import ExitStack

F32 = mybir.dt.float32
BF16 = mybir.dt.bfloat16
FP16 = mybir.dt.float16
U16 = mybir.dt.uint16
I32 = mybir.dt.int32
ALU = mybir.AluOpType
ACT = mybir.ActivationFunctionType

N = 5000
D = 128
P = 128
NT = -(-N // P)
NP = NT * P
CH = 512
NC = NP // CH
TPC = CH // P
HALVES = 2
HC = NC // HALVES
HW = HC * CH
HT = NT // HALVES
CLS = 16
DI = 256
CT = DI // P
ST = 16
RK = 8
KC = 4
LAST_ROWS = N - (NT - 1) * P

SLOTS = 4
GJ = HC
LPC = NT // GJ
VW = CH
RING = 4
SUM_RING = 8
PIECE = 10

PAIRED = [3, 5, 11, 15]
OUT_STEP = 4
H_SCALE = 4096.0

LN_EPS = 1e-5
ROW_EPS = 1e-12
ALPHA = 0.1
N_WEIGHTS = 16

Y_PAIRS = [(0, 0), (0, 1), (1, 0), (1, 1), (0, 2), (1, 2), (2, 0), (2, 1)]


def build(nc, x, h0, adj_t, y_t, gcn_w, gcn_b, ln_g, ln_b, w_in, conv_w, conv_b,
          w_xp, w_dt, b_dt, a_log, d_skip, w_out, out):
    y_parts = nc.dram_tensor("y_parts", (3, CLS, NP), BF16, kind="Internal").ap()

    ctx = ExitStack()
    with ctx:
        def sb(name, shape, dt=F32):
            return ctx.enter_context(nc.sbuf_tensor(name, shape, dt))

        def sem(name):
            return ctx.enter_context(nc.semaphore(name))

        adj_ring = sb("adj_ring", [P, SLOTS, HW])
        x1 = sb("x1", [P, NT, D])
        h1 = sb("h1", [P, NT, D])
        ident = sb("ident", [P, P])
        mean_mat = sb("mean_mat", [P, P])
        ones = sb("ones", [P, 1])
        ln_eps = sb("ln_eps", [P, 1])
        sel32 = sb("sel32", [P, 2 * ST])
        sel = sb("sel", [P, 2 * ST], BF16)
        w_gcn = sb("w_gcn", [P, D])
        b_gcn = sb("b_gcn", [P, 1])
        g_ln = sb("g_ln", [P, 1])
        b_ln = sb("b_ln", [P, 1])
        w_xz = sb("w_xz", [P, 2 * DI])
        w_cv = sb("w_cv", [P, CT, KC])
        b_cv = sb("b_cv", [P, CT])
        w_dbc = sb("w_dbc", [P, CT, P])
        w_dtp = sb("w_dtp", [P, DI])
        b_dtp = sb("b_dtp", [P, CT])
        neg_a = sb("neg_a", [P, CT, ST])
        d_sk = sb("d_sk", [P, CT])
        w_o = sb("w_o", [P, CT, D])
        carry = sb("carry", [P, CT * ST])
        conv_in = sb("conv_in", [P, CT, KC - 1 + CH])
        stats = sb("stats", [P, NT, 6])
        mv = sb("mv", [P, NT, 2])
        rstd = sb("rstd", [P, NT])
        nmr = sb("nmr", [P, NT])
        rinv = sb("rinv", [P, HT])
        rstd_s = sb("rstd_s", [P, NT])
        spare = sb("spare", [P, 6])
        low_sum = sb("low_sum", [P, HALVES * NT])
        low_row = sb("low_row", [P, 1])
        low_all = sb("low_all", [1, 1])

        ARENA = 29184
        arena = sb("arena", [P, ARENA])
        top1 = [0]
        top2 = [0]

        def carve(top, n):
            a = top[0]
            top[0] += n
            assert top[0] <= ARENA, top[0]
            return arena[:, a:a + n]

        def carve1(n):
            return carve(top1, n)

        def carve2(n):
            return carve(top2, n)

        masked = carve1(2 * HW).rearrange("p (b n) -> p b n", b=2)
        magnitude = carve1(2 * HW).rearrange("p (b n) -> p b n", b=2)
        abs_sum = carve1(HW)
        sup_t = carve1(HW).rearrange("p (k n) -> p k n", k=HC)
        y_left = carve1(NP // 2).bitcast(BF16)
        y_right = carve1(NP // 2).bitcast(BF16)
        h0r = carve1(NP).rearrange("p (n d) -> p n d", d=D)
        YW = CLS * NP // P
        y_full = carve1(YW)
        y_rest = carve1(YW)
        low_bits = carve1(HW // 2).bitcast(BF16)
        y_p = [carve1(YW // 2).bitcast(BF16) for _ in range(3)]

        def pair(a):
            return a.rearrange("p (b c n) -> p b c n", b=2, c=CT)

        def tiles(a):
            return a.rearrange("p (c n) -> p c n", c=CT)

        h_hi = carve2(NP // 2).bitcast(FP16).rearrange("p (n d) -> p n d", d=D)
        h_lo = carve2(NP // 2).bitcast(FP16).rearrange("p (n d) -> p n d", d=D)
        u = pair(carve2(2 * CT * CH))
        dt = pair(carve2(2 * CT * CH))
        dtu = tiles(carve2(CT * CH))
        z_gate = pair(carve2(2 * CT * CH))
        buf_a = carve2(CH)
        buf_b = carve2(CH)
        g_t = squares = normed = buf_a
        h_t = log_var = h_ln = buf_b
        centred = carve2(CH)
        z_t = tiles(carve2(CT * CH))
        dt_pos = tiles(carve2(CT * CH))
        conv_out = y_gated = tiles(carve2(CT * CH))
        dbc = buf_a
        bc_rest = buf_b
        bc_hi = centred[:, 0:CH // 2].bitcast(BF16)
        bc_mid = centred[:, CH // 2:CH].bitcast(BF16)
        dt_abs = z_t
        x_out = carve2(CH).rearrange("p (n d) -> p n d", d=D)
        decay = carve2(RING * CH).rearrange("p (b n) -> p b n", b=RING)
        drive = carve2(RING * CH).rearrange("p (b n) -> p b n", b=RING)
        state = carve2(RING * CH).rearrange("p (b n) -> p b n", b=RING)
        state_c = carve2(SUM_RING * CH).rearrange("p (b n) -> p b n", b=SUM_RING)
        b_row = carve2(2 * CH).rearrange("p (b n) -> p b n", b=2)
        bc3 = carve2(CH).bitcast(BF16).rearrange("p (b n) -> p b n", b=2)

        bank = ctx.enter_context(nc.psum_tensor("bank", [P, 8, CH], F32))
        M0, M1, C_BANK, Y_BANK, B_BANK, G_BANK = 0, 1, 2, 4, 6, 7

        x_loaded = [sem(f"x_loaded{i}") for i in range(NT // PIECE)]
        h0_loaded = sem("h0_loaded")
        y_loaded = sem("y_loaded")
        y_split = sem("y_split")
        y_stored = sem("y_stored")
        y_stacked = sem("y_stacked")
        y_stacked_rest = sem("y_stacked_rest")
        w_loaded = sem("w_loaded")
        adj_loaded = [sem(f"adj_loaded{i}") for i in range(SLOTS)]
        const_set = sem("const_set")
        const_step = sem("const_step")
        zeroed = sem("zeroed")
        sel_ready = sem("sel_ready")
        neg_a_ready = sem("neg_a_ready")
        a_exp = sem("a_exp")
        stat_done = sem("stat_done")
        mv_done = sem("mv_done")
        lnv_small = sem("lnv_small")
        rstd_done = sem("rstd_done")
        nmr_done = sem("nmr_done")
        h0r_done = sem("h0r_done")
        x_mixed = sem("x_mixed")
        mask_done = sem("mask_done")
        prod_done = sem("prod_done")
        mag_done = sem("mag_done")
        abs_done = sem("abs_done")
        abs_pool_done = sem("abs_pool_done")
        sup_done = sem("sup_done")
        rows_done = sem("rows_done")
        abs_zeroed = sem("abs_zeroed")
        rinv_step = sem("rinv_step")
        sup_copied = sem("sup_copied")
        turned = sem("turned")
        x1_done = sem("x1_done")
        low_checked = sem("low_checked")
        low_added = sem("low_added")
        low_total = sem("low_total")
        low_known = sem("low_known")
        scaled_done = sem("scaled_done")
        h_hi_done = sem("h_hi_done")
        h_lo_done = sem("h_lo_done")
        paired_done = sem("paired_done")
        h1_done = sem("h1_done")

        g_done = sem("g_done")
        g_copied = sem("g_copied")
        gw_done = sem("gw_done")
        ht_done = sem("ht_done")
        mean_done = sem("mean_done")
        centred_done = sem("centred_done")
        sq_done = sem("sq_done")
        var_done = sem("var_done")
        lnv_done = sem("lnv_done")
        rs_done = sem("rs_done")
        normed_done = sem("normed_done")
        hln_done = sem("hln_done")
        xz_done = sem("xz_done")
        tail_done = sem("tail_done")
        cv_in_done = sem("cv_in_done")
        z_done = sem("z_done")
        zg_done = sem("zg_done")
        conv_step = sem("conv_step")
        u_done = sem("u_done")
        dbc_done = sem("dbc_done")
        dbc_copied = sem("dbc_copied")
        hi_done = sem("hi_done")
        bc3_hi = sem("bc3_hi")
        rest_done = sem("rest_done")
        mid_done = sem("mid_done")
        bc3_mid = sem("bc3_mid")
        bc3_lo = sem("bc3_lo")
        dtw_done = sem("dtw_done")
        dt_abs_done = sem("dt_abs_done")
        dt_pos_done = sem("dt_pos_done")
        dt_log_step = sem("dt_log_step")
        dt_done = sem("dt_done")
        dtu_done = sem("dtu_done")
        b_done = sem("b_done")
        c_done = sem("c_done")
        b_copied = sem("b_copied")
        decay_done = sem("decay_done")
        drive_done = sem("drive_done")
        scan_done = sem("scan_done")
        carried = sem("carried")
        sc_done = sem("sc_done")
        sum_done = sem("sum_done")
        y_mix = sem("y_mix")
        y_gate = sem("y_gate")
        o_done = sem("o_done")
        xo_done = sem("xo_done")
        stored = sem("stored")

        g_used = sem("g_used")
        CARRY0 = CT * ST
        SCAN0 = RING
        SUM0 = SUM_RING
        SC0 = 2
        DRIVE0 = 2
        STORED0 = 16
        X1_0 = 1

        block = ctx.enter_context(nc.Block())

        def over_chunks(eng, body):
            body(0, 0, False, True, True)
            pairs = (NC - 4) // 2
            with eng.Fori(0, pairs) as q:
                for i in range(2):
                    body(2 * q + 1 + i, (1 + i) % 2, True, True, True)
            for c in range(1 + 2 * pairs, NC):
                body(c, c % 2, True, c + 1 < NC, c + 2 < NC)

        def graph_shares():
            other = [2 + 4 * CT * ((s - 2) % ST + 1 not in PAIRED) for s in range(ST)]
            for step, products in ((1, 1), (2, 1), (4, 1 + CT), (6, 2), (7, 2), (11, 2), (12, 2)):
                other[step] += 4 * products
            share = [0] * ST
            for _ in range(NT):
                least = min(range(1, ST), key=lambda s: other[s] + 2 * share[s])
                share[least] += 1
            return share

        share = graph_shares()

        def summed_before(c, i):
            if i < 0:
                n = -sum((j // CT) % ST + 1 not in PAIRED for j in range(CT * ST + i, CT * ST))
            else:
                n = sum(j // CT + 1 not in PAIRED for j in range(i))
            return c * (CT * (ST - len(PAIRED))) + n

        @block.sync
        def _(sp):
            x_v = x.rearrange("(n p) d -> p n d", p=P)
            h0_v = h0.rearrange("(n p) d -> p n d", p=P)
            y_v = y_t.rearrange("c (a m) -> (c a) m", m=YW)
            part_v = y_parts.rearrange("k c (a m) -> k (c a) m", m=YW)
            adj_rows = adj_t.rearrange("(j p) i -> j p i", p=P)
            adj_cols = adj_t.rearrange("(g j p) i -> g p j i", p=P, j=GJ)
            out_v = out[0:(NT - 1) * P, :].rearrange("(n p) d -> p n d", p=P)

            def load_x(i):
                sp.dma_start(x1[:, i * PIECE:(i + 1) * PIECE, :],
                             x_v[:, i * PIECE:(i + 1) * PIECE, :]).then_inc(x_loaded[i], 16)

            def load_row(half, q, r):
                if not (half == 0 and isinstance(q, int) and q == 0):
                    sp.wait_ge(prod_done, HC * (half * NT + q * SLOTS + r - SLOTS + 1))
                    sp.wait_ge(low_checked, half * NT + q * SLOTS + r - SLOTS + 1)
                sp.dma_start(adj_ring[:, r, :], adj_rows[q * SLOTS + r, :, half * HW:(half + 1) * HW]
                             ).then_inc(adj_loaded[r], 16)

            def stack(dst, which, first, last, done):
                parts = [pair[which] for pair in Y_PAIRS]
                for n, k in enumerate(parts):
                    sp.dma_start(dst[n * CLS:(n + 1) * CLS, first:last], y_parts[k, :, first:last]).then_inc(done, 16)

            sp.dma_start(y_full, y_v).then_inc(y_loaded, 16)
            for i in range(3):
                load_x(i)
            sp.wait_ge(y_split, 5)
            for k in range(3):
                sp.dma_start(part_v[k], y_p[k]).then_inc(y_stored, 16)
            load_x(3)
            load_row(0, 0, 0)
            sp.wait_ge(y_stored, 3 * 16)
            stack(y_left, 0, 0, NP, y_stacked)
            stack(y_right, 1, 0, HW, y_stacked)
            for r in range(1, SLOTS):
                load_row(0, 0, r)
            stack(y_right, 1, HW, NP, y_stacked_rest)
            sp.dma_start(h1[:, :, :], h0_v).then_inc(h0_loaded, 16)

            sp.wait_ge(zeroed, 2)
            xp_v = w_xp.rearrange("(t p) n -> p t n", p=P)
            loads = [(w_dbc[:, :, 0:RK], xp_v[:, :, 0:RK])]
            loads += [(w_dbc[:, :, 2 * ST * q:2 * ST * (q + 1)], xp_v[:, :, RK:RK + 2 * ST]) for q in range(1, 4)]
            loads += [(w_dtp[0:RK, :], w_dt), (w_gcn[:], gcn_w), (b_gcn[:], gcn_b), (g_ln[:], ln_g), (b_ln[:], ln_b),
                      (w_xz[:], w_in), (w_cv[:], conv_w.rearrange("(t p) k -> p t k", p=P)),
                      (b_cv[:], conv_b), (b_dtp[:], b_dt), (d_sk[:], d_skip),
                      (neg_a[:], a_log.rearrange("(t p) s -> p t s", p=P)),
                      (w_o[:], w_out.rearrange("(t p) n -> p t n", p=P))]
            assert len(loads) == N_WEIGHTS
            for dst, src in loads:
                sp.dma_start(dst, src).then_inc(w_loaded, 16)
            for half in range(HALVES):
                with sp.Fori(1 if half == 0 else 0, NT // SLOTS) as q:
                    for r in range(SLOTS):
                        load_row(half, q, r)

            def load_cols(k, groups=range(LPC)):
                for g in groups:
                    if isinstance(k, int) and k == 0 and g < SLOTS:
                        sp.wait_ge(prod_done, HC * (HALVES * NT - SLOTS + g + 1))
                        sp.wait_ge(low_checked, HALVES * NT - SLOTS + g + 1)
                    else:
                        sp.wait_ge(g_used, LPC * k + g - SLOTS + 1)
                    sp.dma_start(adj_ring[:, g % SLOTS, :].rearrange("p (j i) -> p j i", j=GJ),
                                 adj_cols[g, :, :, bass.ds(k * CH, CH)]).then_inc(adj_loaded[g % SLOTS], 16)

            def store(c):
                sp.wait_ge(xo_done, c + 1)
                sp.dma_start(out_v[:, bass.ds(c * TPC, TPC), :], x_out).then_inc(stored, 16)

            for k in range(3):
                load_cols(k)
            with sp.Fori(1, NC - 2) as c:
                load_cols(c + 2)
                store(c - 1)
            store(NC - 3)
            store(NC - 2)
            sp.wait_ge(xo_done, NC)
            sp.dma_start(out_v[:, (NC - 1) * TPC:NT - 1, :], x_out[:, 0:TPC - 1, :]).then_inc(stored, 16)
            sp.dma_start(out[(NT - 1) * P:N, :], x_out[0:LAST_ROWS, TPC - 1, :]).then_inc(stored, 16)
            sp.wait_ge(stored, STORED0 + (NC + 1) * 16)

        @block.gpsimd
        def _(pool):
            nc.gpsimd.memset(w_dbc[:], 0.0).then_inc(zeroed, 1)
            nc.gpsimd.memset(w_dtp[:], 0.0).then_inc(zeroed, 1)
            nc.gpsimd.memset(ident[:], 0.0).then_inc(const_step, 1)
            nc.gpsimd.memset(sel32[:], 0.0).then_inc(const_step, 1)
            nc.gpsimd.memset(mean_mat[:], 1.0 / D).then_inc(const_set, 1)
            nc.gpsimd.memset(ones[:], 1.0).then_inc(const_set, 1)
            nc.gpsimd.memset(ln_eps[:], LN_EPS).then_inc(const_set, 1)
            nc.gpsimd.memset(conv_in[:], 0.0).then_inc(const_set, 1)
            pool.wait_ge(const_step, 2)
            nc.gpsimd.affine_select(out=ident[:], in_=ident[:], compare_op=ALU.not_equal, fill=1.0, base=0,
                                    pattern=[[-1, P]], channel_multiplier=1).then_inc(const_set, 1)
            for q in range(1, 4):
                nc.gpsimd.affine_select(out=sel32[:], in_=sel32[:], compare_op=ALU.not_equal, fill=1.0,
                                        base=-2 * ST * q, pattern=[[-1, 2 * ST]],
                                        channel_multiplier=1).then_inc(const_step, 1)
                pool.wait_ge(const_step, 2 + q)
            nc.gpsimd.tensor_copy(sel[:], sel32[:]).then_inc(const_set, 1)
            nc.gpsimd.memset(carry[:], 0.0).then_inc(carried, CARRY0)
            nc.gpsimd.memset(spare[:, 0:1], 0.0).then_inc(scan_done, SCAN0)
            nc.gpsimd.memset(spare[:, 1:2], 0.0).then_inc(sum_done, SUM0)
            nc.gpsimd.memset(spare[:, 2:3], 0.0).then_inc(sc_done, SC0)
            nc.gpsimd.memset(spare[:, 3:4], 0.0).then_inc(drive_done, DRIVE0)
            nc.gpsimd.memset(spare[:, 4:5], 0.0).then_inc(stored, STORED0)
            nc.gpsimd.memset(spare[:, 5:6], 0.0).then_inc(x1_done, X1_0)

            def add_magnitudes(half, q):
                for r in range(SLOTS):
                    tile = half * NT + q * SLOTS + r
                    pool.wait_ge(mag_done, tile + 1)
                    pool.wait_ge(abs_pool_done, tile + half + 1)
                    nc.gpsimd.tensor_tensor(abs_sum[:, VW:HW], magnitude[:, r % 2, VW:HW], abs_sum[:, VW:HW],
                                            ALU.add).then_inc(abs_pool_done, 1)

            for half in range(HALVES):
                if half > 0:
                    pool.wait_ge(rows_done, half)
                nc.gpsimd.memset(abs_sum[:, VW:HW], 0.0).then_inc(abs_pool_done, 1)
                with pool.Fori(0, NT // SLOTS) as q:
                    add_magnitudes(half, q)

            def pre(step, k, pb):
                if step == 11:
                    pool.wait_ge(hi_done, k + 1)
                    pool.wait_ge(dbc_copied, k + 1)
                    nc.gpsimd.tensor_tensor(bc_rest, dbc, bc_hi, ALU.subtract).then_inc(rest_done, 1)
                if step == 12:
                    pool.wait_ge(mid_done, k + 1)
                    if not (isinstance(k, int) and k == 0):
                        pool.wait_ge(carried, CARRY0 + CT * ST * (k - 1) + CT * step)
                    nc.gpsimd.tensor_tensor(bc3[96:128, pb, :], bc_rest[96:128, :], bc_mid[96:128, :],
                                            ALU.subtract).then_inc(bc3_lo, 1)
                    pool.wait_ge(bc3_lo, k + 1)

            def dt_times_u(k, pb):
                pool.wait_ge(dt_done, k + 1)
                pool.wait_ge(u_done, k + 1)
                pool.wait_ge(drive_done, DRIVE0 + CT * ST * k)
                nc.gpsimd.tensor_tensor(dtu, dt[:, pb], u[:, pb], ALU.mult).then_inc(dtu_done, 1)

            def carry_over(v, i):
                pool.wait_ge(scan_done, SCAN0 + v + 1)
                nc.gpsimd.tensor_tensor(carry[:, i:i + 1], state[:, i % RING, CH - 1:CH], ones[:],
                                        ALU.mult).then_inc(carried, 1)

            def body(c, b, do_tail, do_pre, do_gcn):
                pool.wait_ge(dtu_done, c + 1)
                for s in range(ST):
                    for ct in range(CT):
                        i = s * CT + ct
                        v = c * (CT * ST) + i
                        if ct == 0:
                            pool.wait_ge(b_copied, c * ST + s + 1)
                        pool.wait_ge(scan_done, SCAN0 + v - RING + 1)
                        nc.gpsimd.tensor_tensor(drive[:, i % RING, :], dtu[:, ct, :], b_row[:, s % 2, :],
                                                ALU.mult).then_inc(drive_done, 1)
                        if i >= 2:
                            carry_over(v - 2, i - 2)
                    if do_pre:
                        pre(s, c + 1, 1 - b)
                if do_pre:
                    dt_times_u(c + 1, 1 - b)
                for i in range(CT * ST - 2, CT * ST):
                    carry_over(c * (CT * ST) + i, i)

            for s in range(ST):
                pre(s, 0, 0)
            dt_times_u(0, 0)
            over_chunks(pool, body)

        @block.tensor
        def _(pe):
            pe.wait_ge(const_set, 6)
            pe.wait_ge(y_stacked, 2 * len(Y_PAIRS) * 16)

            UNITS = NT * HC
            with pe.Fori(0, HALVES) as half:
                def mask(m):
                    j, k = divmod(m, HC)
                    if m >= 2:
                        pe.wait_ge(prod_done, half * UNITS + m - 1)
                    nc.tensor.matmul(bank[:, 6 + m % 2, :], y_left[:, j * P:(j + 1) * P],
                                     y_right[:, bass.ds(half * HW + k * CH, CH)],
                                     start=True, stop=True).then_inc(mask_done, 1)

                mask(0)
                for m in range(UNITS):
                    j, k = divmod(m, HC)
                    if m + 1 < UNITS:
                        mask(m + 1)
                    if k == 0:
                        pe.wait_ge(h0r_done, j + 1)
                    if j == 0:
                        pe.wait_ge(x1_done, X1_0 + half * TPC * (k + 1))
                    pe.wait_ge(prod_done, half * UNITS + m + 1)
                    nc.tensor.matmul(bank[:, k, :], h0r[:, j, :], masked[:, j % 2, k * CH:(k + 1) * CH],
                                     start=(j == 0), stop=(j == NT - 1)).then_inc(sup_done, 1)
                for k in range(HC):
                    pe.wait_ge(sup_copied, half * HC + k + 1)
                    for i in range(TPC):
                        last = nc.tensor.transpose(bank[:, k, i * P:(i + 1) * P],
                                                   sup_t[:, k, i * P:(i + 1) * P], ident[:])
                    last.then_inc(turned, 1)
                pe.wait_ge(abs_done, half * NT + NT)
                pe.wait_ge(abs_pool_done, (half + 1) * (NT + 1))
                for i in range(HT):
                    last = nc.tensor.matmul(bank[:, 5, i:i + 1], abs_sum[:, i * P:(i + 1) * P], ones[:],
                                            start=True, stop=True)
                last.then_inc(rows_done, 1)
                pe.wait_ge(y_stacked_rest, len(Y_PAIRS) * 16)

            pe.wait_ge(low_added, 1)
            nc.tensor.matmul(bank[0:1, 6, 0:1], low_row[:], ones[:], start=True, stop=True).then_inc(low_total, 1)
            pe.wait_ge(low_known, 1)
            low_bits_sum = pe.value_load(low_all[:].bitcast(I32))

            def k_is_first(k):
                return isinstance(k, int) and k == 0

            def graph(k, tiles_, exact):
                for j in tiles_:
                    g, r = divmod(j, GJ)
                    if j == 0:
                        pe.wait_ge(g_copied, k)
                    if r == 0:
                        pe.wait_ge(adj_loaded[g % SLOTS],
                                   16 * (HALVES * NT // SLOTS + (LPC // SLOTS) * k + g // SLOTS + 1))
                    part = adj_ring[:, g % SLOTS, r * CH:(r + 1) * CH]
                    if exact:
                        if k_is_first(k) and j % PIECE == 0:
                            pe.wait_ge(h_lo_done, j // PIECE + 1)
                        high = part.bitcast(BF16).rearrange("p (n two) -> p n two", two=2)[:, :, 1]
                        nc.tensor.matmul(bank[:, G_BANK, :], h_hi[:, j, :], high, start=(j == 0), stop=False)
                        mm = nc.tensor.matmul(bank[:, G_BANK, :], h_lo[:, j, :], high, start=False,
                                              stop=(j == NT - 1))
                    else:
                        if k_is_first(k) and j % PIECE == 0:
                            pe.wait_ge(h1_done, j + PIECE)
                        mm = nc.tensor.matmul(bank[:, G_BANK, :], h1[:, j, :], part,
                                              start=(j == 0), stop=(j == NT - 1))
                    if r == GJ - 1:
                        mm.then_inc(g_used, 1)

            def pre(step, k, pb):
                if step == 1:
                    pe.wait_ge(g_copied, k + 1)
                    pe.wait_ge(dt_abs_done, CT * k)
                    pe.wait_ge(dt_pos_done, CT * k)
                    nc.tensor.matmul(bank[:, M0, :], w_gcn[:], g_t, start=True, stop=True).then_inc(gw_done, 1)
                if step == 2:
                    pe.wait_ge(ht_done, k + 1)
                    nc.tensor.matmul(bank[:, M1, :], mean_mat[:], h_t, start=True, stop=True).then_inc(mean_done, 1)
                if step == 4:
                    pe.wait_ge(sq_done, k + 1)
                    nc.tensor.matmul(bank[:, M0, :], mean_mat[:], squares, start=True, stop=True).then_inc(var_done, 1)
                if step == 6:
                    pe.wait_ge(hln_done, k + 1)
                    if not k_is_first(k):
                        pe.wait_ge(xo_done, k - 1)
                    for m in range(2):
                        nc.tensor.matmul(bank[:, M0 + m, :], w_xz[:, m * P:(m + 1) * P], h_ln,
                                         start=True, stop=True).then_inc(xz_done, 1)
                if step == 7:
                    for m in range(2):
                        pe.wait_ge(cv_in_done, CT * k + m + 1)
                        nc.tensor.matmul(bank[:, M0 + m, :], w_xz[:, DI + m * P:DI + (m + 1) * P], h_ln,
                                         start=True, stop=True).then_inc(xz_done, 1)
                if step == 11:
                    pe.wait_ge(u_done, k + 1)
                    pe.wait_ge(z_done, CT * k + 1)
                    for t in range(CT):
                        mm = nc.tensor.matmul(bank[:, M0, :], w_dbc[:, t, :], u[:, pb, t, :],
                                              start=(t == 0), stop=(t == CT - 1))
                    mm.then_inc(dbc_done, 1)
                if step == 12:
                    pe.wait_ge(dbc_copied, k + 1)
                    pe.wait_ge(z_done, CT * k + 2)
                    nc.tensor.matmul(bank[:, M1, :], w_dtp[:, 0:P], dbc, start=True, stop=True).then_inc(dtw_done, 1)
                    pe.wait_ge(bc3_hi, k + 1)
                    nc.tensor.matmul(bank[:, M0, :], w_dtp[:, P:DI], dbc, start=True, stop=True).then_inc(dtw_done, 1)

            def second_layer(exact):
                def sums(c, s):
                    for t in range(CT):
                        i = s * CT + t
                        v = c * (CT * ST) + i
                        if s + 1 in PAIRED:
                            continue
                        if i == 0:
                            pe.wait_ge(y_mix, CT * c)
                        if s in PAIRED:
                            pe.wait_ge(paired_done, c * (CT * len(PAIRED)) + PAIRED.index(s) * CT + t + 1)
                        else:
                            pe.wait_ge(sc_done, SC0 + v + 1)
                        nc.tensor.matmul(bank[:, Y_BANK + t, :], ident[:], state_c[:, i % SUM_RING, :],
                                         start=(s == 0), stop=(s == ST - 1)).then_inc(sum_done, 1)

                def spread_b(c, b, s):
                    n = c * ST + s
                    if s == 0:
                        pe.wait_ge(bc3_hi, c + 1)
                        pe.wait_ge(bc3_mid, c + 1)
                        pe.wait_ge(bc3_lo, c + 1)
                    pe.wait_ge(b_copied, n)
                    nc.tensor.matmul(bank[:, B_BANK, :], sel[:, s:s + 1].to_broadcast([P, P]), bc3[:, b, :],
                                     start=True, stop=True).then_inc(b_done, 1)

                def spread_c(c, b, s):
                    pe.wait_ge(sc_done, SC0 + CT * (c * ST + s - 1))
                    nc.tensor.matmul(bank[:, C_BANK + s % 2, :], sel[:, ST + s:ST + s + 1].to_broadcast([P, P]),
                                     bc3[:, b, :], start=True, stop=True).then_inc(c_done, 1)

                def project(c, prepared):
                    pe.wait_ge(y_gate, c + 1)
                    if prepared:
                        pe.wait_ge(centred_done, c + 3)
                    else:
                        pe.wait_ge(dt_abs_done, CT * NC)
                    for i in range(TPC):
                        for t in range(CT):
                            mm = nc.tensor.matmul(bank[:, M1, i * P:(i + 1) * P], y_gated[:, t, i * P:(i + 1) * P],
                                                  w_o[:, t, :], start=(t == 0), stop=(t == CT - 1))
                    mm.then_inc(o_done, 1)

                def body(c, b, do_tail, do_pre, do_gcn):
                    for s in range(ST):
                        if s + 1 < ST:
                            spread_b(c, b, s + 1)
                        elif do_pre:
                            spread_b(c + 1, 1 - b, 0)
                        if do_gcn and s > 0:
                            graph(c + 2, range(sum(share[:s]), sum(share[:s + 1])), exact)
                        if do_pre:
                            pre(s, c + 1, 1 - b)
                        if s >= 2:
                            sums(c, s - 2)
                        elif do_tail:
                            sums(c - 1, ST - 2 + s)
                        if do_tail and s == OUT_STEP:
                            project(c - 1, do_pre)
                        if s + 1 < ST:
                            spread_c(c, b, s + 1)
                        elif do_pre:
                            spread_c(c + 1, 1 - b, 0)

                graph(0, range(NT), exact)
                pe.wait_ge(g_copied, 1)
                per_step = NT // ST + 1
                for s in range(ST):
                    graph(1, range(min(NT, s * per_step), min(NT, (s + 1) * per_step)), exact)
                    pre(s, 0, 0)
                spread_b(0, 0, 0)
                spread_c(0, 0, 0)
                over_chunks(pe, body)
                sums(NC - 1, ST - 2)
                sums(NC - 1, ST - 1)
                project(NC - 1, False)

            pe.wait_ge(w_loaded, N_WEIGHTS * 16)
            with pe.If(low_bits_sum == 0):
                second_layer(True)
            with pe.Else():
                second_layer(False)

        @block.scalar
        def _(act):
            act.preload_act_table_set("natural_log_exp_and_others")
            act.wait_ge(const_set, 3)

            def rstd_group(g, n, at):
                act.wait_ge(mv_done, g + 1)
                act.activation(rstd[:, at:at + n], mv[:, at:at + n, 1], ACT.Ln, bias=ln_eps[:]).then_inc(lnv_small, 1)
                act.wait_ge(lnv_small, g + 1)
                act.activation(rstd[:, at:at + n], rstd[:, at:at + n], ACT.Exp, scale=-0.5).then_inc(rstd_done, 1)

            def relu_group(g, tiles_, src, dst, done, scale):
                act.wait_ge(nmr_done, g + 1)
                for i in tiles_:
                    act.activation(dst[:, i, :], src[:, i, :], ACT.Relu,
                                   bias=nmr[:, i:i + 1], scale=scale[:, i:i + 1]).then_inc(done, 1)

            groups = NT // PIECE
            rstd_group(0, PIECE, 0)
            relu_group(0, range(PIECE), x1, h0r, h0r_done, rstd)
            for g in range(1, groups):
                rstd_group(g, PIECE, g * PIECE)
            for g in range(1, groups):
                relu_group(g, range(g * PIECE, (g + 1) * PIECE), x1, h0r, h0r_done, rstd)

            def magnitudes(half, q, r):
                tile = half * NT + q * SLOTS + r
                act.wait_ge(adj_loaded[r], 16 * (half * (NT // SLOTS) + q + 1))
                act.wait_ge(low_checked, tile)
                act.activation(low_bits, adj_ring[:, r, :].bitcast(U16).rearrange("p (n two) -> p n two", two=2)[:, :, 0],
                               ACT.Copy, accum_out=low_sum[:, bass.ds(tile, 1)]).then_inc(low_checked, 1)
                act.wait_ge(prod_done, HC * (tile + 1))
                if not (isinstance(q, int) and half == 0 and r < 2):
                    act.wait_ge(abs_done, tile - 1)
                    act.wait_ge(abs_pool_done, tile + half)
                act.activation(magnitude[:, r % 2, :], masked[:, r % 2, :], ACT.Abs).then_inc(mag_done, 1)

            for half in range(HALVES):
                for r in range(SLOTS):
                    magnitudes(half, 0, r)
                    if half > 0 and r == 0:
                        rstd_group(groups + half - 1, HT, (half - 1) * HT)
                    if half > 0 and r >= 1:
                        a, b = (HT * (r - 1) // (SLOTS - 1), HT * r // (SLOTS - 1))
                        relu_group(groups + half - 1, range((half - 1) * HT + a, (half - 1) * HT + b),
                                   x1, h1, h1_done, rstd_s)
                with act.Fori(1, NT // SLOTS) as q:
                    for r in range(SLOTS):
                        magnitudes(half, q, r)
                for k in range(HC):
                    act.wait_ge(sup_done, (half + 1) * NT * HC - HC + k + 1)
                    act.activation(sup_t[:, k, :], bank[:, k, :], ACT.Copy).then_inc(sup_copied, 1)

            def to_fp16(pieces):
                for i in pieces:
                    act.wait_ge(h1_done, (i + 1) * PIECE)
                    act.activation(h_hi[:, i * PIECE:(i + 1) * PIECE, :], h1[:, i * PIECE:(i + 1) * PIECE, :],
                                   ACT.Copy).then_inc(h_hi_done, 1)

            act.wait_ge(mag_done, HALVES * NT)
            to_fp16(range(groups // 2))
            rstd_group(groups + HALVES - 1, HT, NT - HT)
            for g in range(groups // 2, groups):
                relu_group(groups + HALVES - 1, range(g * PIECE, (g + 1) * PIECE), x1, h1, h1_done, rstd_s)
                to_fp16([g])

            act.wait_ge(w_loaded, N_WEIGHTS * 16)
            act.activation(neg_a[:], neg_a[:], ACT.Exp).then_inc(a_exp, 1)
            act.wait_ge(a_exp, 1)
            act.activation(neg_a[:], neg_a[:], ACT.Copy, scale=-1.0).then_inc(neg_a_ready, 1)
            act.wait_ge(neg_a_ready, 1)

            def pre(step, k, pb):
                if step == 0:
                    act.wait_ge(g_used, LPC * (k + 1))
                    act.activation(g_t, bank[:, G_BANK, :], ACT.Copy, scale=1.0 / H_SCALE).then_inc(g_copied, 1)
                if step == 1:
                    act.wait_ge(gw_done, k + 1)
                    act.activation(h_t, bank[:, M0, :], ACT.Relu, bias=b_gcn[:]).then_inc(ht_done, 1)
                if step == 3:
                    act.wait_ge(centred_done, k + 1)
                    act.activation(squares, centred, ACT.Square).then_inc(sq_done, 1)
                if step == 4:
                    act.wait_ge(var_done, k + 1)
                    act.activation(log_var, bank[:, M0, :], ACT.Ln, bias=ln_eps[:]).then_inc(lnv_done, 1)
                    act.wait_ge(lnv_done, k + 1)
                    act.activation(log_var, log_var, ACT.Exp, scale=-0.5).then_inc(rs_done, 1)
                if step == 5:
                    act.wait_ge(normed_done, k + 1)
                    act.activation(h_ln, normed, ACT.Identity, bias=b_ln[:]).then_inc(hln_done, 1)
                if step == 6:
                    act.wait_ge(conv_step, CT * KC * k)
                    act.activation(conv_in[:, :, 0:KC - 1], conv_in[:, :, CH:CH + KC - 1], ACT.Copy).then_inc(tail_done, 1)
                    act.wait_ge(tail_done, k + 1)
                    for t in range(CT):
                        act.wait_ge(xz_done, 2 * CT * k + t + 1)
                        act.activation(conv_in[:, t, KC - 1:], bank[:, M0 + t, :], ACT.Copy).then_inc(cv_in_done, 1)
                if step == 7:
                    for t in range(CT):
                        act.wait_ge(xz_done, 2 * CT * k + CT + t + 1)
                        act.activation(z_t[:, t, :], bank[:, M0 + t, :], ACT.Copy).then_inc(z_done, 1)
                if step == 10:
                    act.preload_act_table_set("silu_and_others")
                    if not (isinstance(k, int) and k == 0):
                        act.wait_ge(y_gate, k - 1)
                    act.wait_ge(z_done, CT * (k + 1))
                    act.activation(z_gate[:, pb], z_t, ACT.Silu).then_inc(zg_done, 1)
                    act.wait_ge(conv_step, CT * KC * (k + 1))
                    act.activation(u[:, pb], conv_out, ACT.Silu).then_inc(u_done, 1)
                    act.preload_act_table_set("natural_log_exp_and_others")
                if step == 11:
                    act.wait_ge(dbc_done, k + 1)
                    act.activation(bc_hi, bank[:, M0, :], ACT.Copy).then_inc(hi_done, 1)
                    act.activation(dbc, bank[:, M0, :], ACT.Copy).then_inc(dbc_copied, 1)
                    act.activation(bc3[0:64, pb, :], bank[0:64, M0, :], ACT.Copy).then_inc(bc3_hi, 1)
                if step == 12:
                    act.wait_ge(rest_done, k + 1)
                    act.activation(bc_mid, bc_rest, ACT.Copy).then_inc(mid_done, 1)
                    act.activation(bc3[64:96, pb, :], bc_rest[64:96, :], ACT.Copy).then_inc(bc3_mid, 1)
                if step == 13:
                    act.wait_ge(zg_done, k + 1)
                    for t in range(CT):
                        act.wait_ge(dtw_done, CT * k + t + 1)
                        act.activation(dt_pos[:, t, :], bank[:, M1 - t, :], ACT.Relu,
                                       bias=b_dtp[:, t:t + 1]).then_inc(dt_pos_done, 1)
                        act.activation(dt_abs[:, t, :], bank[:, M1 - t, :], ACT.Abs,
                                       bias=b_dtp[:, t:t + 1]).then_inc(dt_abs_done, 1)
                    act.wait_ge(dt_abs_done, CT * (k + 1))
                    act.activation(dt_abs, dt_abs, ACT.Exp, scale=-1.0).then_inc(dt_log_step, 1)
                    act.wait_ge(dt_log_step, 2 * k + 1)
                    act.activation(dt_abs, dt_abs, ACT.Ln, bias=ones[:]).then_inc(dt_log_step, 1)

            def copy_b(c, s):
                n = c * ST + s
                act.wait_ge(b_done, n + 1)
                act.wait_ge(drive_done, DRIVE0 + CT * (n - 1))
                act.activation(b_row[:, s % 2, :], bank[:, B_BANK, :], ACT.Copy).then_inc(b_copied, 1)

            def body(c, b, do_tail, do_pre, do_gcn):
                act.wait_ge(dt_done, c + 1)
                for s in range(ST):
                    for t in range(CT):
                        i = s * CT + t
                        v = c * (CT * ST) + i
                        act.wait_ge(scan_done, SCAN0 + v - RING + 1)
                        act.activation(decay[:, i % RING, :], dt[:, b, t, :], ACT.Exp,
                                       scale=neg_a[:, t, s:s + 1]).then_inc(decay_done, 1)
                    if s + 1 < ST:
                        copy_b(c, s + 1)
                    elif do_pre:
                        copy_b(c + 1, 0)
                    if do_pre:
                        pre(s, c + 1, 1 - b)

            for s in range(ST):
                pre(s, 0, 0)
            copy_b(0, 0)
            over_chunks(act, body)

        @block.vector
        def _(dve):
            dve.wait_ge(y_loaded, 16)
            nc.vector.tensor_copy(y_p[0], y_full).then_inc(y_split, 1)
            dve.wait_ge(y_split, 1)
            nc.vector.tensor_tensor(y_rest, y_full, y_p[0], ALU.subtract).then_inc(y_split, 1)
            dve.wait_ge(y_split, 2)
            nc.vector.tensor_copy(y_p[1], y_rest).then_inc(y_split, 1)
            dve.wait_ge(y_split, 3)
            nc.vector.tensor_tensor(y_rest, y_rest, y_p[1], ALU.subtract).then_inc(y_split, 1)
            dve.wait_ge(y_split, 4)
            nc.vector.tensor_copy(y_p[2], y_rest).then_inc(y_split, 1)

            def stat_group(g, src, n, first, at, base):
                for i in range(n):
                    nc.vector.bn_stats(stats[:, at + i, :], src[:, first + i, :]).then_inc(stat_done, 1)
                for i in range(n):
                    dve.wait_ge(stat_done, base + i + 1)
                    agg = nc.vector.bn_aggr(mv[:, at + i, :], stats[:, at + i, :])
                agg.then_inc(mv_done, 1)

            def nmr_group(g, n, at, scale=rstd):
                dve.wait_ge(rstd_done, g + 1)
                if scale is rstd_s:
                    nc.vector.tensor_scalar(rstd_s[:, at:at + n], rstd[:, at:at + n], H_SCALE, None,
                                            ALU.mult).then_inc(scaled_done, 1)
                    dve.wait_ge(scaled_done, g - groups + 1)
                nc.vector.scalar_tensor_tensor(nmr[:, at:at + n], mv[:, at:at + n, 0], -1.0, scale[:, at:at + n],
                                               ALU.mult, ALU.mult).then_inc(nmr_done, 1)

            groups = NT // PIECE

            def x_stats(g):
                dve.wait_ge(x_loaded[g], 16)
                stat_group(g, x1, PIECE, g * PIECE, g * PIECE, g * PIECE)

            x_stats(0)
            nmr_group(0, PIECE, 0)
            x_stats(1)
            for g in range(1, groups):
                if g + 1 < groups:
                    x_stats(g + 1)
                nmr_group(g, PIECE, g * PIECE)

            def mix(n):
                nc.vector.scalar_tensor_tensor(x1[:, bass.ds(n, 1), :], h1[:, bass.ds(n, 1), :], ALPHA,
                                               x1[:, bass.ds(n, 1), :], ALU.mult, ALU.add).then_inc(x_mixed, 1)

            def mask_group(half, q, first):
                for r in range(SLOTS):
                    tile = half * NT + q * SLOTS + r
                    dve.wait_ge(adj_loaded[r], 16 * (half * (NT // SLOTS) + q + 1))
                    if not (first and r < 2):
                        dve.wait_ge(sup_done, HC * (tile - 1))
                        dve.wait_ge(mag_done, tile - 1)
                    for k in range(HC):
                        dve.wait_ge(mask_done, HC * tile + k + 1)
                        nc.vector.tensor_tensor(masked[:, r % 2, k * CH:(k + 1) * CH], bank[:, 6 + (r + k) % 2, :],
                                                adj_ring[:, r, k * CH:(k + 1) * CH], ALU.mult).then_inc(prod_done, 1)
                    if not (first and r == 0):
                        add_magnitudes(tile - 1, (r - 1) % 2)
                    if half == 0 and not first:
                        mix((q - 1) * SLOTS + r)
                    if half > 0 and first and r == 0:
                        stat_group(groups + half - 1, x1, HT, (half - 1) * HT, (half - 1) * HT,
                                   NT + (half - 1) * HT)
                    if half > 0 and first and r == 1:
                        nmr_group(groups + half - 1, HT, (half - 1) * HT, rstd_s)

            def add_magnitudes(tile, slot):
                dve.wait_ge(mag_done, tile + 1)
                dve.wait_ge(abs_done, tile)
                nc.vector.tensor_tensor(abs_sum[:, 0:VW], magnitude[:, slot, 0:VW], abs_sum[:, 0:VW],
                                        ALU.add).then_inc(abs_done, 1)

            def x1_half(half):
                dve.wait_ge(rows_done, half + 1)
                nc.vector.tensor_scalar(rinv[:], bank[:, 5, 0:HT], ROW_EPS, None, ALU.max).then_inc(rinv_step, 1)
                dve.wait_ge(rinv_step, 3 * half + 1)
                nc.vector.reciprocal(rinv[:], rinv[:]).then_inc(rinv_step, 1)
                dve.wait_ge(rinv_step, 3 * half + 2)
                nc.vector.tensor_scalar(rinv[:], rinv[:], 1.0 - ALPHA, None, ALU.mult).then_inc(rinv_step, 1)
                dve.wait_ge(rinv_step, 3 * half + 3)
                dve.wait_ge(x_mixed, NT)
                for n in range(HT):
                    k, i = divmod(n, TPC)
                    if i == 0:
                        dve.wait_ge(turned, half * HC + k + 1)
                    nc.vector.scalar_tensor_tensor(x1[:, half * HT + n, :], bank[:, k, i * P:(i + 1) * P],
                                                   rinv[:, n:n + 1], x1[:, half * HT + n, :],
                                                   ALU.mult, ALU.add).then_inc(x1_done, 1)
                dve.wait_ge(x1_done, X1_0 + (half + 1) * HT)

            for half in range(HALVES):
                if half > 0:
                    x1_half(half - 1)
                nc.vector.memset(abs_sum[:, 0:VW], 0.0).then_inc(abs_zeroed, 1)
                dve.wait_ge(abs_zeroed, half + 1)
                mask_group(half, 0, True)
                if half == 0:
                    dve.wait_ge(h0_loaded, 16)
                    dve.wait_ge(h0r_done, NT)
                with dve.Fori(1, NT // SLOTS) as q:
                    mask_group(half, q, False)
                if half == 0:
                    for n in range(NT - SLOTS, NT):
                        mix(n)
                add_magnitudes(half * NT + NT - 1, 1)

            dve.wait_ge(low_checked, HALVES * NT)
            nc.vector.reduce_sum(low_row[:], low_sum[:], axis=mybir.AxisListType.X).then_inc(low_added, 1)

            def h_rest(pieces):
                for i in pieces:
                    dve.wait_ge(h_hi_done, i + 1)
                    nc.vector.tensor_tensor(h_lo[:, i * PIECE:(i + 1) * PIECE, :], h1[:, i * PIECE:(i + 1) * PIECE, :],
                                            h_hi[:, i * PIECE:(i + 1) * PIECE, :], ALU.subtract).then_inc(h_lo_done, 1)

            h_rest(range(groups // 2))
            dve.wait_ge(low_total, 1)
            nc.vector.tensor_copy(low_all[:], bank[0:1, 6, 0:1]).then_inc(low_known, 1)
            x1_half(HALVES - 1)
            stat_group(groups + HALVES - 1, x1, HT, NT - HT, NT - HT, 2 * NT - HT)
            nmr_group(groups + HALVES - 1, HT, NT - HT, rstd_s)
            h_rest(range(groups // 2, groups))

            def pre(step, k, pb):
                if step == 2:
                    dve.wait_ge(mean_done, k + 1)
                    nc.vector.tensor_tensor(centred, h_t, bank[:, M1, :], ALU.subtract).then_inc(centred_done, 1)
                if step == 4:
                    dve.wait_ge(rs_done, k + 1)
                    nc.vector.scalar_tensor_tensor(normed, centred, g_ln[:], log_var, ALU.mult,
                                                   ALU.mult).then_inc(normed_done, 1)
                if step in (6, 7, 8, 9):
                    t, first = divmod(KC // 2 * (step - 6), KC)
                    if first == 0:
                        dve.wait_ge(cv_in_done, CT * k + t + 1)
                    if first == 0 and t == 0:
                        dve.wait_ge(u_done, k)
                        if not (isinstance(k, int) and k == 0):
                            dve.wait_ge(o_done, k - 1)
                    for j in range(first, first + KC // 2):
                        if j == 0:
                            nc.vector.tensor_scalar(conv_out[:, t, :], conv_in[:, t, 0:CH], w_cv[:, t, 0:1],
                                                    b_cv[:, t:t + 1], ALU.mult, ALU.add).then_inc(conv_step, 1)
                        else:
                            dve.wait_ge(conv_step, CT * KC * k + KC * t + j)
                            nc.vector.scalar_tensor_tensor(conv_out[:, t, :], conv_in[:, t, j:j + CH],
                                                           w_cv[:, t, j:j + 1], conv_out[:, t, :],
                                                           ALU.mult, ALU.add).then_inc(conv_step, 1)
                if step == 13:
                    dve.wait_ge(dt_log_step, 2 * (k + 1))
                    dve.wait_ge(dt_pos_done, CT * (k + 1))
                    nc.vector.tensor_tensor(dt[:, pb], dt_pos, dt_abs, ALU.add).then_inc(dt_done, 1)

            def tail(step, c, b):
                if step == 1:
                    if isinstance(c, int) and c == NC - 1:
                        dve.wait_ge(u_done, NC)
                        dve.wait_ge(o_done, NC - 1)
                    else:
                        dve.wait_ge(u_done, c + 2)
                    for t in range(CT):
                        dve.wait_ge(sum_done, SUM0 + summed_before(c, CT * ST) - CT + t + 1)
                        nc.vector.scalar_tensor_tensor(y_gated[:, t, :], u[:, b, t, :], d_sk[:, t:t + 1],
                                                       bank[:, Y_BANK + t, :], ALU.mult, ALU.add).then_inc(y_mix, 1)
                if step == 2:
                    dve.wait_ge(y_mix, CT * (c + 1))
                    nc.vector.tensor_tensor(y_gated, y_gated, z_gate[:, b], ALU.mult).then_inc(y_gate, 1)
                if step == OUT_STEP + 1:
                    dve.wait_ge(o_done, c + 1)
                    dve.wait_ge(stored, STORED0 + 16 * c)
                    nc.vector.tensor_tensor(x_out, bank[:, M1, :].rearrange("p (n d) -> p n d", d=D),
                                            x1[:, bass.ds(c * TPC, TPC), :], ALU.add).then_inc(xo_done, 1)

            def body(c, b, do_tail, do_pre, do_gcn):
                def times_c(i):
                    v = c * (CT * ST) + i
                    dve.wait_ge(c_done, c * ST + i // CT + 1)
                    dve.wait_ge(scan_done, SCAN0 + v + 1)
                    dve.wait_ge(sum_done, SUM0 + summed_before(c, i - SUM_RING + 1))
                    nc.vector.tensor_tensor(state_c[:, i % SUM_RING, :], state[:, i % RING, :],
                                            bank[:, C_BANK + (i // CT) % 2, :], ALU.mult).then_inc(sc_done, 1)
                    if i // CT in PAIRED:
                        dve.wait_ge(sc_done, SC0 + v + 1)
                        nc.vector.tensor_tensor(state_c[:, i % SUM_RING, :], state_c[:, i % SUM_RING, :],
                                                state_c[:, (i - CT) % SUM_RING, :], ALU.add).then_inc(paired_done, 1)

                for s in range(ST):
                    for t in range(CT):
                        i = s * CT + t
                        v = c * (CT * ST) + i
                        dve.wait_ge(decay_done, v + 1)
                        dve.wait_ge(drive_done, DRIVE0 + v + 1)
                        dve.wait_ge(carried, CARRY0 + v - RING + 1)
                        nc.vector.tensor_tensor_scan(state[:, i % RING, :], decay[:, i % RING, :],
                                                     drive[:, i % RING, :], carry[:, i:i + 1],
                                                     ALU.mult, ALU.add).then_inc(scan_done, 1)
                        if i > 0:
                            times_c(i - 1)
                    if do_tail:
                        tail(s, c - 1, 1 - b)
                    if do_pre:
                        pre(s, c + 1, 1 - b)
                times_c(CT * ST - 1)

            for s in range(ST):
                pre(s, 0, 0)
            over_chunks(dve, body)
            for s in range(ST):
                tail(s, NC - 1, (NC - 1) % 2)


def kernel(x, adj, L0_gnn_h0, L0_gnn_y, L1_gnn_gcn_w, L1_gnn_gcn_b, L1_gnn_ln_g, L1_gnn_ln_b, L1_gnn_w_in,
           L1_gnn_conv_w, L1_gnn_conv_b, L1_gnn_w_xp, L1_gnn_w_dt, L1_gnn_b_dt, L1_gnn_A_log, L1_gnn_D_skip,
           L1_gnn_w_out):
    import numpy as np
    import concourse.bacc as bacc
    from concourse.bass_utils import run_bass_kernel_spmd

    def rows(a):
        a = np.asarray(a)
        return np.concatenate([a, np.zeros((NP - N,) + a.shape[1:], a.dtype)])

    def columns(a):
        return np.ascontiguousarray(np.asarray(a).reshape(-1, P).T)

    adj_t = np.zeros((NP, NP), np.asarray(adj).dtype)
    adj_t[:N, :N] = np.asarray(adj).T
    y_t = np.ascontiguousarray(rows(L0_gnn_y).T)
    arrays = [("x", rows(x)), ("h0", rows(L0_gnn_h0)), ("adj_t", adj_t), ("y_t", y_t),
              ("gcn_w", L1_gnn_gcn_w), ("gcn_b", columns(L1_gnn_gcn_b)), ("ln_g", columns(L1_gnn_ln_g)),
              ("ln_b", columns(L1_gnn_ln_b)), ("w_in", L1_gnn_w_in), ("conv_w", L1_gnn_conv_w),
              ("conv_b", columns(L1_gnn_conv_b)), ("w_xp", L1_gnn_w_xp), ("w_dt", L1_gnn_w_dt),
              ("b_dt", columns(L1_gnn_b_dt)), ("a_log", L1_gnn_A_log), ("d_skip", columns(L1_gnn_D_skip)),
              ("w_out", L1_gnn_w_out)]
    nc = bacc.Bacc("TRN2", target_bir_lowering=False, num_devices=1)
    feed, args = {}, []
    for name, a in arrays:
        a = np.ascontiguousarray(a)
        feed[f"in_{name}"] = a
        args.append(nc.dram_tensor(f"in_{name}", a.shape, mybir.dt.from_np(a.dtype), kind="ExternalInput").ap())
    out = nc.dram_tensor("out_x", (N, D), F32, kind="ExternalOutput").ap()
    build(nc, *args, out)
    r = run_bass_kernel_spmd(nc, [feed], core_ids=[0])
    return r.results[0]["out_x"]
```

```python
import concourse.bass as bass
from concourse import mybir
from contextlib import ExitStack

F32 = mybir.dt.float32
BF16 = mybir.dt.bfloat16
FP16 = mybir.dt.float16
U16 = mybir.dt.uint16
I32 = mybir.dt.int32
ALU = mybir.AluOpType
ACT = mybir.ActivationFunctionType

N = 5000
D = 128
P = 128
NT = -(-N // P)
NP = NT * P
CH = 512
NC = NP // CH
TPC = CH // P
HALVES = 2
HC = NC // HALVES
HW = HC * CH
HT = NT // HALVES
CLS = 16
DI = 256
CT = DI // P
ST = 16
RK = 8
KC = 4
LAST_ROWS = N - (NT - 1) * P

SLOTS = 4
GJ = 2
LPC = NT // GJ
VW = CH
VW_LAST = 3 * CH
RING = 8
STATE_RING = 4
B_RING = 4
SUM_RING = 8
PIECE = 10
GROUPS = NT // PIECE

DVE_PAIRED = [2, 10, 14]
POOL_PAIRED = [5, 8]
PAIRED = DVE_PAIRED + POOL_PAIRED
CONV_STEPS = [7, 8]
OUT_STEP = 3
H_SCALE = 4096.0

LN_EPS = 1e-5
ROW_EPS = 1e-12
ALPHA = 0.1
N_WEIGHTS = 16

Y_PAIRS = [(0, 0), (0, 1), (1, 0), (1, 1), (0, 2), (1, 2), (2, 0), (2, 1)]


def build(nc, x, h0, adj_t, y_t, gcn_w, gcn_b, ln_g, ln_b, w_in, conv_w, conv_b,
          w_xp, w_dt, b_dt, a_log, d_skip, w_out, out):
    y_parts = nc.dram_tensor("y_parts", (3, CLS, NP), BF16, kind="Internal").ap()

    ctx = ExitStack()
    with ctx:
        def sb(name, shape, dt=F32):
            return ctx.enter_context(nc.sbuf_tensor(name, shape, dt))

        def sem(name):
            return ctx.enter_context(nc.semaphore(name))

        adj_ring = sb("adj_ring", [P, SLOTS, HW])
        x1 = sb("x1", [P, NT, D])
        h1 = sb("h1", [P, NT, D])
        ident = sb("ident", [P, P])
        mean_mat = sb("mean_mat", [P, P])
        ones = sb("ones", [P, CT])
        ln_eps = sb("ln_eps", [P, 1])
        sel32 = sb("sel32", [P, 2 * ST])
        sel = sb("sel", [P, 2 * ST], BF16)
        w_gcn = sb("w_gcn", [P, D])
        b_gcn = sb("b_gcn", [P, 1])
        g_ln = sb("g_ln", [P, 1])
        b_ln = sb("b_ln", [P, 1])
        w_xz = sb("w_xz", [P, 2 * DI])
        w_cv = sb("w_cv", [P, CT, KC])
        b_cv = sb("b_cv", [P, CT])
        w_dbc = sb("w_dbc", [P, CT, P])
        w_dtp = sb("w_dtp", [P, DI])
        b_dtp = sb("b_dtp", [P, CT])
        neg_a = sb("neg_a", [P, CT, ST])
        d_sk = sb("d_sk", [P, CT])
        w_o = sb("w_o", [P, CT, D])
        carry = sb("carry", [P, CT * ST])
        conv_in = sb("conv_in", [P, CT, KC - 1 + CH])
        stats = sb("stats", [P, NT, 6])
        mv = sb("mv", [P, NT, 2])
        rstd = sb("rstd", [P, NT])
        nmr = sb("nmr", [P, NT])
        rinv = sb("rinv", [P, HT])
        rstd_s = sb("rstd_s", [P, NT])
        spare = sb("spare", [P, 6])
        low_sum = sb("low_sum", [P, HALVES * NT])
        low_row = sb("low_row", [P, 1])
        low_all = sb("low_all", [1, 1])

        ARENA = 29184
        arena = sb("arena", [P, ARENA])
        top1 = [0]
        top2 = [0]

        def carve(top, n):
            a = top[0]
            top[0] += n
            assert top[0] <= ARENA, top[0]
            return arena[:, a:a + n]

        def carve1(n):
            return carve(top1, n)

        def carve2(n):
            return carve(top2, n)

        masked = carve1(2 * HW).rearrange("p (b n) -> p b n", b=2)
        magnitude = carve1(2 * HW).rearrange("p (b n) -> p b n", b=2)
        abs_sum = carve1(HW)
        sup_t = carve1(HW).rearrange("p (k n) -> p k n", k=HC)
        y_left = carve1(NP // 2).bitcast(BF16)
        y_right = carve1(NP // 2).bitcast(BF16)
        h0r = carve1(NP).rearrange("p (n d) -> p n d", d=D)
        YW = CLS * NP // P
        y_full = carve1(YW)
        y_rest = carve1(YW)
        low_bits = carve1(HW // 2).bitcast(BF16)
        y_p = [carve1(YW // 2).bitcast(BF16) for _ in range(3)]

        def pair(a):
            return a.rearrange("p (b c n) -> p b c n", b=2, c=CT)

        def tiles(a):
            return a.rearrange("p (c n) -> p c n", c=CT)

        h_hi = carve2(NP // 2).bitcast(FP16).rearrange("p (n d) -> p n d", d=D)
        h_lo = carve2(NP // 2).bitcast(FP16).rearrange("p (n d) -> p n d", d=D)
        u = pair(carve2(2 * CT * CH))
        dt = pair(carve2(2 * CT * CH))
        z_gate = pair(carve2(2 * CT * CH))
        buf_a = carve2(CH)
        buf_b = carve2(CH)
        g_t = squares = normed = buf_a
        h_t = log_var = h_ln = buf_b
        centred = carve2(CH)
        z_t = tiles(carve2(CT * CH))
        dt_pos = tiles(carve2(CT * CH))
        conv_out = y_gated = tiles(carve2(CT * CH))
        dbc = buf_a
        bc_rest = buf_b
        bc_hi = centred[:, 0:CH // 2].bitcast(BF16)
        bc_mid = centred[:, CH // 2:CH].bitcast(BF16)
        dt_abs = z_t
        x_out = carve2(CH).rearrange("p (n d) -> p n d", d=D)
        decay = carve2(RING * CH).rearrange("p (b n) -> p b n", b=RING)
        state = carve2(STATE_RING * CH).rearrange("p (b n) -> p b n", b=STATE_RING)
        state_c = carve2(SUM_RING * CH).rearrange("p (b n) -> p b n", b=SUM_RING)
        adj_flat = adj_ring.rearrange("p s n -> p (s n)")
        col_ring = adj_flat[:, 0:SLOTS * GJ * CH].rearrange("p (s n) -> p s n", s=SLOTS)
        at = SLOTS * GJ * CH
        drive = adj_flat[:, at:at + RING * CH].rearrange("p (b n) -> p b n", b=RING)
        at += RING * CH
        b_row = adj_flat[:, at:at + B_RING * CH].rearrange("p (b n) -> p b n", b=B_RING)
        assert at + B_RING * CH <= SLOTS * HW
        dtu = tiles(carve2(CT * CH))
        bc3 = carve2(CH).bitcast(BF16).rearrange("p (b n) -> p b n", b=2)

        bank = ctx.enter_context(nc.psum_tensor("bank", [P, 8, CH], F32))
        M0, M1, C_BANK, Y_BANK, B_BANK, G_BANK = 0, 1, 2, 4, 6, 7

        x_loaded = [sem(f"x_loaded{i}") for i in range(NT // PIECE)]
        h0_loaded = sem("h0_loaded")
        y_loaded = sem("y_loaded")
        y_split = sem("y_split")
        y_stored = sem("y_stored")
        y_stacked = sem("y_stacked")
        y_left_stacked = sem("y_left_stacked")
        y_right_stacked = sem("y_right_stacked")
        w_loaded = sem("w_loaded")
        adj_loaded = [sem(f"adj_loaded{i}") for i in range(SLOTS)]
        const_set = sem("const_set")
        const_step = sem("const_step")
        zeroed = sem("zeroed")
        neg_a_ready = sem("neg_a_ready")
        a_exp = sem("a_exp")
        stat_done = sem("stat_done")
        mv_done = sem("mv_done")
        lnv_small = sem("lnv_small")
        rstd_done = sem("rstd_done")
        nmr_done = sem("nmr_done")
        h0r_done = sem("h0r_done")
        x_mixed = sem("x_mixed")
        mask_done = sem("mask_done")
        prod_done = sem("prod_done")
        mag_done = sem("mag_done")
        abs_done = sem("abs_done")
        abs_pool_done = sem("abs_pool_done")
        sup_done = sem("sup_done")
        rows_done = sem("rows_done")
        abs_zeroed = sem("abs_zeroed")
        rinv_step = sem("rinv_step")
        sup_copied = sem("sup_copied")
        turned = sem("turned")
        x1_done = sem("x1_done")
        low_checked = sem("low_checked")
        low_added = sem("low_added")
        low_total = sem("low_total")
        low_known = sem("low_known")
        scaled_done = sem("scaled_done")
        h_hi_done = sem("h_hi_done")
        h_lo_done = sem("h_lo_done")
        paired_done = sem("paired_done")
        pool_paired = sem("pool_paired")
        h1_done = sem("h1_done")

        g_copied = sem("g_copied")
        gw_done = sem("gw_done")
        ht_done = sem("ht_done")
        mean_done = sem("mean_done")
        centred_done = sem("centred_done")
        sq_done = sem("sq_done")
        var_done = sem("var_done")
        lnv_done = sem("lnv_done")
        rs_done = sem("rs_done")
        normed_done = sem("normed_done")
        hln_done = sem("hln_done")
        xz_done = sem("xz_done")
        tail_done = sem("tail_done")
        cv_in_done = sem("cv_in_done")
        z_done = sem("z_done")
        zg_done = sem("zg_done")
        tap_done = sem("tap_done")
        conv_step = sem("conv_step")
        u_done = sem("u_done")
        dbc_done = sem("dbc_done")
        dbc_copied = sem("dbc_copied")
        hi_done = sem("hi_done")
        bc3_hi = sem("bc3_hi")
        rest_done = sem("rest_done")
        mid_done = sem("mid_done")
        bc3_mid = sem("bc3_mid")
        bc3_lo = sem("bc3_lo")
        dtw_done = sem("dtw_done")
        dt_abs_done = sem("dt_abs_done")
        dt_pos_done = sem("dt_pos_done")
        dt_log_step = sem("dt_log_step")
        dt_done = sem("dt_done")
        dtu_done = sem("dtu_done")
        b_done = sem("b_done")
        c_done = sem("c_done")
        b_copied = sem("b_copied")
        decay_done = sem("decay_done")
        drive_done = sem("drive_done")
        scan_done = sem("scan_done")
        carried = sem("carried")
        sc_done = sem("sc_done")
        sum_done = sem("sum_done")
        y_mix = sem("y_mix")
        y_gate = sem("y_gate")
        o_done = sem("o_done")
        xo_done = sem("xo_done")
        stored = sem("stored")

        g_used = sem("g_used")
        CARRY0 = CT * ST
        SCAN0 = RING
        SUM0 = SUM_RING
        SC0 = 2
        DRIVE0 = CT * (B_RING - 1)
        STORED0 = 16
        X1_0 = 1

        block = ctx.enter_context(nc.Block())

        def over_chunks(eng, body):
            body(0, 0, False, True, True)
            pairs = (NC - 4) // 2
            with eng.Fori(0, pairs) as q:
                for i in range(2):
                    body(2 * q + 1 + i, (1 + i) % 2, True, True, True)
            for c in range(1 + 2 * pairs, NC):
                body(c, c % 2, True, c + 1 < NC, c + 2 < NC)

        def graph_shares():
            other = [2 + 4 * CT * ((s - 2) % ST + 1 not in PAIRED) for s in range(ST)]
            for step, products in ((1, 1), (2, 1), (OUT_STEP, CT), (4, 1), (6, 2), (7, 2), (10, 2), (11, 2)):
                other[step] += 4 * products
            share = [0] * ST
            for _ in range(NT):
                least = min(range(1, ST), key=lambda s: other[s] + 2 * share[s])
                share[least] += 1
            return share

        share = graph_shares()

        def ahead(s, do_pre):
            if s + 2 < ST:
                return [(0, s + 2)]
            return [(1, 0), (1, 1)] if s == ST - 1 and do_pre else []

        UNPAIRED_FROM = NC - 2

        def paired(c, states=PAIRED):
            return [] if isinstance(c, int) and c >= UNPAIRED_FROM else states

        def summed_before(c, i):
            def terms(c, first, last):
                return sum(j // CT + 1 not in paired(c) for j in range(first, last))

            before = min(c, UNPAIRED_FROM) if isinstance(c, int) else c
            n = before * (CT * (ST - len(PAIRED)))
            if isinstance(c, int) and c > UNPAIRED_FROM:
                n += (c - UNPAIRED_FROM) * CT * ST
            return n - terms(c - 1, CT * ST + i, CT * ST) if i < 0 else n + terms(c, 0, i)

        @block.sync
        def _(sp):
            x_v = x.rearrange("(n p) d -> p n d", p=P)
            h0_v = h0.rearrange("(n p) d -> p n d", p=P)
            y_v = y_t.rearrange("c (a m) -> (c a) m", m=YW)
            part_v = y_parts.rearrange("k c (a m) -> k (c a) m", m=YW)
            adj_rows = adj_t.rearrange("(j p) i -> j p i", p=P)
            adj_cols = adj_t.rearrange("(g j p) i -> g p j i", p=P, j=GJ)
            out_v = out[0:(NT - 1) * P, :].rearrange("(n p) d -> p n d", p=P)

            def load_x(i):
                sp.dma_start(x1[:, i * PIECE:(i + 1) * PIECE, :],
                             x_v[:, i * PIECE:(i + 1) * PIECE, :]).then_inc(x_loaded[i], 16)

            def load_row(half, q, r):
                if not (half == 0 and isinstance(q, int) and q == 0):
                    sp.wait_ge(prod_done, HC * (half * NT + q * SLOTS + r - SLOTS + 1))
                    sp.wait_ge(low_checked, half * NT + q * SLOTS + r - SLOTS + 1)
                sp.dma_start(adj_ring[:, r, :], adj_rows[q * SLOTS + r, :, half * HW:(half + 1) * HW]
                             ).then_inc(adj_loaded[r], 16)

            def stack(dst, which, first, last, done):
                parts = [pair[which] for pair in Y_PAIRS]
                for n, k in enumerate(parts):
                    sp.dma_start(dst[n * CLS:(n + 1) * CLS, first:last], y_parts[k, :, first:last]).then_inc(done, 16)

            sp.dma_start(y_full, y_v).then_inc(y_loaded, 16)
            for i in range(3):
                load_x(i)
            sp.wait_ge(y_split, 5)
            for k in range(3):
                sp.dma_start(part_v[k], y_p[k]).then_inc(y_stored, 16)
            load_x(3)
            load_row(0, 0, 0)
            sp.wait_ge(y_stored, 3 * 16)
            stack(y_left, 0, 0, PIECE * P, y_stacked)
            stack(y_right, 1, 0, HW, y_stacked)
            for r in range(1, SLOTS):
                load_row(0, 0, r)
            stack(y_left, 0, PIECE * P, NP, y_left_stacked)
            stack(y_right, 1, HW, NP, y_right_stacked)
            sp.dma_start(h1[:, :, :], h0_v).then_inc(h0_loaded, 16)

            sp.wait_ge(zeroed, 2)
            xp_v = w_xp.rearrange("(t p) n -> p t n", p=P)
            loads = [(w_dbc[:, :, 0:RK], xp_v[:, :, 0:RK])]
            loads += [(w_dbc[:, :, 2 * ST * q:2 * ST * (q + 1)], xp_v[:, :, RK:RK + 2 * ST]) for q in range(1, 4)]
            loads += [(w_dtp[0:RK, :], w_dt), (w_gcn[:], gcn_w), (b_gcn[:], gcn_b), (g_ln[:], ln_g), (b_ln[:], ln_b),
                      (w_xz[:], w_in), (w_cv[:], conv_w.rearrange("(t p) k -> p t k", p=P)),
                      (b_cv[:], conv_b), (b_dtp[:], b_dt), (d_sk[:], d_skip),
                      (neg_a[:], a_log.rearrange("(t p) s -> p t s", p=P)),
                      (w_o[:], w_out.rearrange("(t p) n -> p t n", p=P))]
            assert len(loads) == N_WEIGHTS
            for dst, src in loads:
                sp.dma_start(dst, src).then_inc(w_loaded, 16)
            for half in range(HALVES):
                with sp.Fori(1 if half == 0 else 0, NT // SLOTS) as q:
                    for r in range(SLOTS):
                        load_row(half, q, r)

            def load_cols(k, groups=range(LPC)):
                for g in groups:
                    if isinstance(k, int) and k == 0 and g < SLOTS:
                        sp.wait_ge(prod_done, HC * (HALVES * NT - SLOTS + g + 1))
                        sp.wait_ge(low_checked, HALVES * NT - SLOTS + g + 1)
                    else:
                        sp.wait_ge(g_used, LPC * k + g - SLOTS + 1)
                    sp.dma_start(col_ring[:, g % SLOTS, :].rearrange("p (j i) -> p j i", j=GJ),
                                 adj_cols[g, :, :, bass.ds(k * CH, CH)]).then_inc(adj_loaded[g % SLOTS], 16)

            def store(c):
                sp.wait_ge(xo_done, c + 1)
                sp.dma_start(out_v[:, bass.ds(c * TPC, TPC), :], x_out).then_inc(stored, 16)

            for k in range(3):
                load_cols(k)
            with sp.Fori(1, NC - 2) as c:
                load_cols(c + 2)
                store(c - 1)
            store(NC - 3)
            store(NC - 2)
            sp.wait_ge(xo_done, NC)
            sp.dma_start(out_v[:, (NC - 1) * TPC:NT - 1, :], x_out[:, 0:TPC - 1, :]).then_inc(stored, 16)
            sp.dma_start(out[(NT - 1) * P:N, :], x_out[0:LAST_ROWS, TPC - 1, :]).then_inc(stored, 16)
            sp.wait_ge(stored, STORED0 + (NC + 1) * 16)

        @block.gpsimd
        def _(pool):
            nc.gpsimd.memset(w_dbc[:], 0.0).then_inc(zeroed, 1)
            nc.gpsimd.memset(w_dtp[:], 0.0).then_inc(zeroed, 1)
            nc.gpsimd.memset(ident[:], 0.0).then_inc(const_step, 1)
            nc.gpsimd.memset(sel32[:], 0.0).then_inc(const_step, 1)
            nc.gpsimd.memset(mean_mat[:], 1.0 / D).then_inc(const_set, 1)
            nc.gpsimd.memset(ones[:], 1.0).then_inc(const_set, 1)
            nc.gpsimd.memset(ln_eps[:], LN_EPS).then_inc(const_set, 1)
            nc.gpsimd.memset(conv_in[:], 0.0).then_inc(const_set, 1)
            pool.wait_ge(const_step, 2)
            nc.gpsimd.affine_select(out=ident[:], in_=ident[:], compare_op=ALU.not_equal, fill=1.0, base=0,
                                    pattern=[[-1, P]], channel_multiplier=1).then_inc(const_set, 1)
            for q in range(1, 4):
                nc.gpsimd.affine_select(out=sel32[:], in_=sel32[:], compare_op=ALU.not_equal, fill=1.0,
                                        base=-2 * ST * q, pattern=[[-1, 2 * ST]],
                                        channel_multiplier=1).then_inc(const_step, 1)
                pool.wait_ge(const_step, 2 + q)
            nc.gpsimd.tensor_copy(sel[:], sel32[:]).then_inc(const_set, 1)
            nc.gpsimd.memset(carry[:], 0.0).then_inc(carried, CARRY0)
            nc.gpsimd.memset(spare[:, 0:1], 0.0).then_inc(scan_done, SCAN0)
            nc.gpsimd.memset(spare[:, 1:2], 0.0).then_inc(sum_done, SUM0)
            nc.gpsimd.memset(spare[:, 2:3], 0.0).then_inc(sc_done, SC0)
            nc.gpsimd.memset(spare[:, 3:4], 0.0).then_inc(drive_done, DRIVE0)
            nc.gpsimd.memset(spare[:, 4:5], 0.0).then_inc(stored, STORED0)
            nc.gpsimd.memset(spare[:, 5:6], 0.0).then_inc(x1_done, X1_0)

            def add_magnitudes(half, q):
                for r in range(SLOTS):
                    tile = half * NT + q * SLOTS + r
                    first = VW_LAST if isinstance(q, int) and r == SLOTS - 1 else VW
                    pool.wait_ge(mag_done, tile + 1)
                    pool.wait_ge(abs_pool_done, tile + half + 1)
                    nc.gpsimd.tensor_tensor(abs_sum[:, first:HW], magnitude[:, r % 2, first:HW], abs_sum[:, first:HW],
                                            ALU.add).then_inc(abs_pool_done, 1)

            for half in range(HALVES):
                if half > 0:
                    pool.wait_ge(rows_done, half)
                nc.gpsimd.memset(abs_sum[:, VW:HW], 0.0).then_inc(abs_pool_done, 1)
                with pool.Fori(0, NT // SLOTS - 1) as q:
                    add_magnitudes(half, q)
                add_magnitudes(half, NT // SLOTS - 1)

            def pre(step, k, pb):
                if step == 12:
                    pool.wait_ge(hi_done, k + 1)
                    pool.wait_ge(dbc_copied, k + 1)
                    nc.gpsimd.tensor_tensor(bc_rest, dbc, bc_hi, ALU.subtract).then_inc(rest_done, 1)
                if step == 14:
                    pool.wait_ge(mid_done, k + 1)
                    if not (isinstance(k, int) and k == 0):
                        pool.wait_ge(carried, CARRY0 + CT * ST * (k - 1) + CT * step)
                    nc.gpsimd.tensor_tensor(bc3[96:128, pb, :], bc_rest[96:128, :], bc_mid[96:128, :],
                                            ALU.subtract).then_inc(bc3_lo, 1)
                    pool.wait_ge(bc3_lo, k + 1)

            def dt_times_u(k, pb, t):
                pool.wait_ge(dt_done, k + 1)
                pool.wait_ge(u_done, k + 1)
                pool.wait_ge(drive_done, DRIVE0 + CT * ST * k)
                nc.gpsimd.tensor_tensor(dtu[:, t, :], dt[:, pb, t, :], u[:, pb, t, :], ALU.mult).then_inc(dtu_done, 1)

            def carry_over(c, s):
                i = s * CT
                pool.wait_ge(scan_done, SCAN0 + c * (CT * ST) + i + CT)
                nc.gpsimd.tensor_tensor(carry[:, i:i + CT], state[:, i % STATE_RING:i % STATE_RING + CT, CH - 1],
                                        ones[:, 0:CT], ALU.mult).then_inc(carried, CT)

            def body(c, b, do_tail, do_pre, do_gcn):
                for s in range(ST):
                    for ct in range(CT):
                        i = s * CT + ct
                        v = c * (CT * ST) + i
                        if s == 0:
                            if ct > 0:
                                dt_times_u(c, b, ct)
                            pool.wait_ge(dtu_done, CT * c + ct + 1)
                        if ct == 0:
                            pool.wait_ge(b_copied, c * ST + s + 1)
                        pool.wait_ge(scan_done, SCAN0 + v - RING + 1)
                        nc.gpsimd.tensor_tensor(drive[:, i % RING, :], dtu[:, ct, :], b_row[:, s % B_RING, :],
                                                ALU.mult).then_inc(drive_done, 1)
                    if s >= 1:
                        carry_over(c, s - 1)
                    elif do_tail:
                        carry_over(c - 1, ST - 1)
                    if s - 2 in paired(c, POOL_PAIRED):
                        for t in range(CT):
                            i = (s - 2) * CT + t
                            if t == 0:
                                pool.wait_ge(sc_done, SC0 + c * (CT * ST) + i + CT)
                            nc.gpsimd.tensor_tensor(state_c[:, i % SUM_RING, :], state_c[:, i % SUM_RING, :],
                                                    state_c[:, (i - CT) % SUM_RING, :], ALU.add).then_inc(pool_paired, 1)
                    if do_pre:
                        pre(s, c + 1, 1 - b)
                if do_pre:
                    dt_times_u(c + 1, 1 - b, 0)

            for s in range(ST):
                pre(s, 0, 0)
            dt_times_u(0, 0, 0)
            over_chunks(pool, body)

        @block.tensor
        def _(pe):
            pe.wait_ge(const_set, 6)
            pe.wait_ge(y_stacked, 2 * len(Y_PAIRS) * 16)

            UNITS = NT * HC
            with pe.Fori(0, HALVES) as half:
                def mask(m):
                    j, k = divmod(m, HC)
                    if m == PIECE * HC:
                        pe.wait_ge(y_left_stacked, len(Y_PAIRS) * 16)
                    if m >= 2:
                        pe.wait_ge(prod_done, half * UNITS + m - 1)
                    nc.tensor.matmul(bank[:, 6 + m % 2, :], y_left[:, j * P:(j + 1) * P],
                                     y_right[:, bass.ds(half * HW + k * CH, CH)],
                                     start=True, stop=True).then_inc(mask_done, 1)

                mask(0)
                for m in range(UNITS):
                    j, k = divmod(m, HC)
                    if m + 1 < UNITS:
                        mask(m + 1)
                    if k == 0:
                        pe.wait_ge(h0r_done, j + 1)
                    if j == 0:
                        pe.wait_ge(x1_done, X1_0 + half * TPC * (k + 1))
                    pe.wait_ge(prod_done, half * UNITS + m + 1)
                    nc.tensor.matmul(bank[:, k, :], h0r[:, j, :], masked[:, j % 2, k * CH:(k + 1) * CH],
                                     start=(j == 0), stop=(j == NT - 1)).then_inc(sup_done, 1)
                for k in range(HC):
                    pe.wait_ge(sup_copied, half * HC + k + 1)
                    for i in range(TPC):
                        last = nc.tensor.transpose(bank[:, k, i * P:(i + 1) * P],
                                                   sup_t[:, k, i * P:(i + 1) * P], ident[:])
                    last.then_inc(turned, 1)
                pe.wait_ge(abs_done, half * NT + NT)
                for i in range(HT):
                    if i == VW_LAST // P:
                        pe.wait_ge(abs_pool_done, (half + 1) * (NT + 1))
                    last = nc.tensor.matmul(bank[:, 5, i:i + 1], abs_sum[:, i * P:(i + 1) * P], ones[:, 0:1],
                                            start=True, stop=True)
                last.then_inc(rows_done, 1)
                pe.wait_ge(y_right_stacked, len(Y_PAIRS) * 16)

            pe.wait_ge(low_added, 1)
            nc.tensor.matmul(bank[0:1, 6, 0:1], low_row[:], ones[:, 0:1], start=True, stop=True).then_inc(low_total, 1)
            pe.wait_ge(low_known, 1)
            low_bits_sum = pe.value_load(low_all[:].bitcast(I32))

            def k_is_first(k):
                return isinstance(k, int) and k == 0

            def graph(k, tiles_, exact):
                for j in tiles_:
                    g, r = divmod(j, GJ)
                    if j == 0:
                        pe.wait_ge(g_copied, k)
                    if r == 0:
                        pe.wait_ge(adj_loaded[g % SLOTS],
                                   16 * (HALVES * NT // SLOTS + (LPC // SLOTS) * k + g // SLOTS + 1))
                    part = col_ring[:, g % SLOTS, r * CH:(r + 1) * CH]
                    if exact:
                        if k_is_first(k) and j % PIECE == 0:
                            pe.wait_ge(h_lo_done, j // PIECE + 1)
                        high = part.bitcast(BF16).rearrange("p (n two) -> p n two", two=2)[:, :, 1]
                        nc.tensor.matmul(bank[:, G_BANK, :], h_hi[:, j, :], high, start=(j == 0), stop=False)
                        mm = nc.tensor.matmul(bank[:, G_BANK, :], h_lo[:, j, :], high, start=False,
                                              stop=(j == NT - 1))
                    else:
                        if k_is_first(k) and j % PIECE == 0:
                            pe.wait_ge(h1_done, j + PIECE)
                        mm = nc.tensor.matmul(bank[:, G_BANK, :], h1[:, j, :], part,
                                              start=(j == 0), stop=(j == NT - 1))
                    if r == GJ - 1:
                        mm.then_inc(g_used, 1)

            def pre(step, k, pb):
                if step == 1:
                    pe.wait_ge(g_copied, k + 1)
                    pe.wait_ge(dt_abs_done, CT * k)
                    pe.wait_ge(dt_pos_done, CT * k)
                    nc.tensor.matmul(bank[:, M0, :], w_gcn[:], g_t, start=True, stop=True).then_inc(gw_done, 1)
                if step == 2:
                    pe.wait_ge(ht_done, k + 1)
                    nc.tensor.matmul(bank[:, M1, :], mean_mat[:], h_t, start=True, stop=True).then_inc(mean_done, 1)
                if step == 4:
                    pe.wait_ge(sq_done, k + 1)
                    nc.tensor.matmul(bank[:, M0, :], mean_mat[:], squares, start=True, stop=True).then_inc(var_done, 1)
                if step == 6:
                    pe.wait_ge(hln_done, k + 1)
                    if not k_is_first(k):
                        pe.wait_ge(xo_done, k - 1)
                    for m in range(2):
                        nc.tensor.matmul(bank[:, M0 + m, :], w_xz[:, m * P:(m + 1) * P], h_ln,
                                         start=True, stop=True).then_inc(xz_done, 1)
                if step == 7:
                    for m in range(2):
                        pe.wait_ge(cv_in_done, CT * k + m + 1)
                        nc.tensor.matmul(bank[:, M0 + m, :], w_xz[:, DI + m * P:DI + (m + 1) * P], h_ln,
                                         start=True, stop=True).then_inc(xz_done, 1)
                if step == 10:
                    pe.wait_ge(u_done, k + 1)
                    pe.wait_ge(z_done, CT * k + 1)
                    for t in range(CT):
                        mm = nc.tensor.matmul(bank[:, M0, :], w_dbc[:, t, :], u[:, pb, t, :],
                                              start=(t == 0), stop=(t == CT - 1))
                    mm.then_inc(dbc_done, 1)
                if step == 11:
                    pe.wait_ge(dbc_copied, k + 1)
                    pe.wait_ge(z_done, CT * k + 2)
                    nc.tensor.matmul(bank[:, M1, :], w_dtp[:, 0:P], dbc, start=True, stop=True).then_inc(dtw_done, 1)
                    pe.wait_ge(bc3_hi, k + 1)
                    nc.tensor.matmul(bank[:, M0, :], w_dtp[:, P:DI], dbc, start=True, stop=True).then_inc(dtw_done, 1)

            def second_layer(exact):
                def sums(c, s):
                    for t in range(CT):
                        i = s * CT + t
                        v = c * (CT * ST) + i
                        if s + 1 in paired(c):
                            continue
                        if s == 0 and not k_is_first(c):
                            pe.wait_ge(y_mix, CT * (c - 1) + t + 1)
                        if s in paired(c, DVE_PAIRED):
                            pe.wait_ge(paired_done, (c * len(DVE_PAIRED) + DVE_PAIRED.index(s)) * CT + t + 1)
                        elif s in paired(c, POOL_PAIRED):
                            pe.wait_ge(pool_paired, (c * len(POOL_PAIRED) + POOL_PAIRED.index(s)) * CT + t + 1)
                        else:
                            pe.wait_ge(sc_done, SC0 + v + 1)
                        nc.tensor.matmul(bank[:, Y_BANK + t, :], ident[:], state_c[:, i % SUM_RING, :],
                                         start=(s == 0), stop=(s == ST - 1)).then_inc(sum_done, 1)

                def spread_b(c, b, s):
                    n = c * ST + s
                    if s == 0:
                        pe.wait_ge(bc3_hi, c + 1)
                        pe.wait_ge(bc3_mid, c + 1)
                        pe.wait_ge(bc3_lo, c + 1)
                    pe.wait_ge(b_copied, n)
                    nc.tensor.matmul(bank[:, B_BANK, :], sel[:, s:s + 1].to_broadcast([P, P]), bc3[:, b, :],
                                     start=True, stop=True).then_inc(b_done, 1)

                def spread_c(c, b, s):
                    pe.wait_ge(sc_done, SC0 + CT * (c * ST + s - 1))
                    nc.tensor.matmul(bank[:, C_BANK + s % 2, :], sel[:, ST + s:ST + s + 1].to_broadcast([P, P]),
                                     bc3[:, b, :], start=True, stop=True).then_inc(c_done, 1)

                def project(c, prepared):
                    pe.wait_ge(y_gate, c + 1)
                    if prepared:
                        pe.wait_ge(centred_done, c + 3)
                    else:
                        pe.wait_ge(dt_abs_done, CT * NC)
                    for i in range(TPC):
                        for t in range(CT):
                            mm = nc.tensor.matmul(bank[:, M1, i * P:(i + 1) * P], y_gated[:, t, i * P:(i + 1) * P],
                                                  w_o[:, t, :], start=(t == 0), stop=(t == CT - 1))
                    mm.then_inc(o_done, 1)

                def body(c, b, do_tail, do_pre, do_gcn):
                    for s in range(ST):
                        rows_ahead = ahead(s, do_pre)
                        for on, state_ in rows_ahead[:1]:
                            spread_b(c + on, (b + on) % 2, state_)
                        if do_gcn and s > 0:
                            graph(c + 2, range(sum(share[:s]), sum(share[:s + 1])), exact)
                        if do_pre:
                            pre(s, c + 1, 1 - b)
                        if s >= 2:
                            sums(c, s - 2)
                        elif do_tail:
                            sums(c - 1, ST - 2 + s)
                        if do_tail and s == OUT_STEP:
                            project(c - 1, do_pre)
                        if s + 1 < ST:
                            spread_c(c, b, s + 1)
                        elif do_pre:
                            spread_c(c + 1, 1 - b, 0)
                        for on, state_ in rows_ahead[1:]:
                            spread_b(c + on, (b + on) % 2, state_)

                graph(0, range(NT), exact)
                pe.wait_ge(g_copied, 1)
                per_step = NT // ST + 1
                for s in range(ST):
                    graph(1, range(min(NT, s * per_step), min(NT, (s + 1) * per_step)), exact)
                    pre(s, 0, 0)
                spread_b(0, 0, 0)
                spread_c(0, 0, 0)
                spread_b(0, 0, 1)
                over_chunks(pe, body)
                sums(NC - 1, ST - 2)
                sums(NC - 1, ST - 1)
                project(NC - 1, False)

            pe.wait_ge(w_loaded, N_WEIGHTS * 16)
            with pe.If(low_bits_sum == 0):
                second_layer(True)
            with pe.Else():
                second_layer(False)

        @block.scalar
        def _(act):
            act.preload_act_table_set("natural_log_exp_and_others")
            act.wait_ge(const_set, 3)

            def rstd_group(g):
                n, at = PIECE, PIECE * (g % GROUPS)
                act.wait_ge(mv_done, g + 1)
                act.activation(rstd[:, at:at + n], mv[:, at:at + n, 1], ACT.Ln, bias=ln_eps[:]).then_inc(lnv_small, 1)
                act.wait_ge(lnv_small, g + 1)
                act.activation(rstd[:, at:at + n], rstd[:, at:at + n], ACT.Exp, scale=-0.5).then_inc(rstd_done, 1)

            def relu_group(g, tiles_, src, dst, done, scale):
                act.wait_ge(nmr_done, g + 1)
                for i in tiles_:
                    act.activation(dst[:, i, :], src[:, i, :], ACT.Relu,
                                   bias=nmr[:, i:i + 1], scale=scale[:, i:i + 1]).then_inc(done, 1)

            rstd_group(0)
            relu_group(0, range(PIECE), x1, h0r, h0r_done, rstd)
            for g in range(1, GROUPS):
                rstd_group(g)
            for g in range(1, GROUPS):
                relu_group(g, range(g * PIECE, (g + 1) * PIECE), x1, h0r, h0r_done, rstd)

            def magnitudes(half, q, r):
                tile = half * NT + q * SLOTS + r
                act.wait_ge(adj_loaded[r], 16 * (half * (NT // SLOTS) + q + 1))
                act.wait_ge(low_checked, tile)
                act.activation(low_bits, adj_ring[:, r, :].bitcast(U16).rearrange("p (n two) -> p n two", two=2)[:, :, 0],
                               ACT.Copy, accum_out=low_sum[:, bass.ds(tile, 1)]).then_inc(low_checked, 1)
                act.wait_ge(prod_done, HC * (tile + 1))
                if not (isinstance(q, int) and half == 0 and r < 2):
                    act.wait_ge(abs_done, tile - 1)
                    act.wait_ge(abs_pool_done, tile + half)
                act.activation(magnitude[:, r % 2, :], masked[:, r % 2, :], ACT.Abs).then_inc(mag_done, 1)

            for half in range(HALVES):
                peeled = 1 if half == 0 else 2
                for tile in range(peeled * SLOTS):
                    magnitudes(half, tile // SLOTS, tile % SLOTS)
                    if half > 0 and tile in (1, 2):
                        rstd_group(GROUPS + tile - 1)
                    if half > 0 and tile >= 3:
                        share = HT // (2 * SLOTS - 3)
                        first = (tile - 3) * share
                        relu_group(GROUPS + (first + share - 1) // PIECE, range(first, first + share),
                                   x1, h1, h1_done, rstd_s)
                with act.Fori(peeled, NT // SLOTS) as q:
                    for r in range(SLOTS):
                        magnitudes(half, q, r)
                for k in range(HC):
                    act.wait_ge(sup_done, (half + 1) * NT * HC - HC + k + 1)
                    act.activation(sup_t[:, k, :], bank[:, k, :], ACT.Copy).then_inc(sup_copied, 1)

            def to_fp16(pieces):
                for i in pieces:
                    act.wait_ge(h1_done, (i + 1) * PIECE)
                    act.activation(h_hi[:, i * PIECE:(i + 1) * PIECE, :], h1[:, i * PIECE:(i + 1) * PIECE, :],
                                   ACT.Copy).then_inc(h_hi_done, 1)

            act.wait_ge(mag_done, HALVES * NT)
            to_fp16(range(GROUPS // 2))
            for g in range(GROUPS // 2, GROUPS):
                rstd_group(GROUPS + g)
                relu_group(GROUPS + g, range(g * PIECE, (g + 1) * PIECE), x1, h1, h1_done, rstd_s)
                to_fp16([g])

            act.wait_ge(w_loaded, N_WEIGHTS * 16)
            act.activation(neg_a[:], neg_a[:], ACT.Exp).then_inc(a_exp, 1)
            act.wait_ge(a_exp, 1)
            act.activation(neg_a[:], neg_a[:], ACT.Copy, scale=-1.0).then_inc(neg_a_ready, 1)
            act.wait_ge(neg_a_ready, 1)

            def pre(step, k, pb):
                if step == 0:
                    act.wait_ge(g_used, LPC * (k + 1))
                    act.activation(g_t, bank[:, G_BANK, :], ACT.Copy, scale=1.0 / H_SCALE).then_inc(g_copied, 1)
                if step == 1:
                    act.wait_ge(gw_done, k + 1)
                    act.activation(h_t, bank[:, M0, :], ACT.Relu, bias=b_gcn[:]).then_inc(ht_done, 1)
                if step == 3:
                    act.wait_ge(centred_done, k + 1)
                    act.activation(squares, centred, ACT.Square).then_inc(sq_done, 1)
                if step == 4:
                    act.wait_ge(var_done, k + 1)
                    act.activation(log_var, bank[:, M0, :], ACT.Ln, bias=ln_eps[:]).then_inc(lnv_done, 1)
                    act.wait_ge(lnv_done, k + 1)
                    act.activation(log_var, log_var, ACT.Exp, scale=-0.5).then_inc(rs_done, 1)
                if step == 5:
                    act.wait_ge(normed_done, k + 1)
                    act.activation(h_ln, normed, ACT.Identity, bias=b_ln[:]).then_inc(hln_done, 1)
                if step == 6:
                    act.wait_ge(conv_step, CT * (KC - 1) * k)
                    act.activation(conv_in[:, :, 0:KC - 1], conv_in[:, :, CH:CH + KC - 1], ACT.Copy).then_inc(tail_done, 1)
                    act.wait_ge(tail_done, k + 1)
                    for t in range(CT):
                        act.wait_ge(xz_done, 2 * CT * k + t + 1)
                        act.activation(conv_in[:, t, KC - 1:], bank[:, M0 + t, :], ACT.Copy).then_inc(cv_in_done, 1)
                    act.wait_ge(u_done, k)
                    if not (isinstance(k, int) and k == 0):
                        act.wait_ge(o_done, k - 1)
                    for t in range(CT):
                        act.wait_ge(cv_in_done, CT * k + t + 1)
                        act.activation(conv_out[:, t, :], conv_in[:, t, 0:CH], ACT.Identity, bias=b_cv[:, t:t + 1],
                                       scale=w_cv[:, t, 0:1]).then_inc(tap_done, 1)
                if step == 7:
                    for t in range(CT):
                        act.wait_ge(xz_done, 2 * CT * k + CT + t + 1)
                        act.activation(z_t[:, t, :], bank[:, M0 + t, :], ACT.Copy).then_inc(z_done, 1)
                if step == 9:
                    act.preload_act_table_set("silu_and_others")
                    if not (isinstance(k, int) and k == 0):
                        act.wait_ge(y_gate, k - 1)
                    act.wait_ge(conv_step, CT * (KC - 1) * (k + 1))
                    act.activation(u[:, pb], conv_out, ACT.Silu).then_inc(u_done, 1)
                    act.wait_ge(z_done, CT * (k + 1))
                    act.activation(z_gate[:, pb], z_t, ACT.Silu).then_inc(zg_done, 1)
                    act.preload_act_table_set("natural_log_exp_and_others")
                if step == 10:
                    act.wait_ge(dbc_done, k + 1)
                    act.activation(bc_hi, bank[:, M0, :], ACT.Copy).then_inc(hi_done, 1)
                    act.activation(dbc, bank[:, M0, :], ACT.Copy).then_inc(dbc_copied, 1)
                    act.activation(bc3[0:64, pb, :], bank[0:64, M0, :], ACT.Copy).then_inc(bc3_hi, 1)
                if step == 13:
                    act.wait_ge(rest_done, k + 1)
                    act.activation(bc_mid, bc_rest, ACT.Copy).then_inc(mid_done, 1)
                    act.activation(bc3[64:96, pb, :], bc_rest[64:96, :], ACT.Copy).then_inc(bc3_mid, 1)
                if step == 12:
                    act.wait_ge(zg_done, k + 1)
                    for t in range(CT):
                        act.wait_ge(dtw_done, CT * k + t + 1)
                        act.activation(dt_pos[:, t, :], bank[:, M1 - t, :], ACT.Relu,
                                       bias=b_dtp[:, t:t + 1]).then_inc(dt_pos_done, 1)
                        act.activation(dt_abs[:, t, :], bank[:, M1 - t, :], ACT.Abs,
                                       bias=b_dtp[:, t:t + 1]).then_inc(dt_abs_done, 1)
                if step == 13:
                    act.wait_ge(dt_abs_done, CT * (k + 1))
                    act.activation(dt_abs, dt_abs, ACT.Exp, scale=-1.0).then_inc(dt_log_step, 1)
                    act.wait_ge(dt_log_step, 2 * k + 1)
                    act.activation(dt_abs, dt_abs, ACT.Ln, bias=ones[:, 0:1]).then_inc(dt_log_step, 1)

            def copy_b(c, s):
                n = c * ST + s
                act.wait_ge(b_done, n + 1)
                act.wait_ge(drive_done, DRIVE0 + CT * (n - B_RING + 1))
                act.activation(b_row[:, s % B_RING, :], bank[:, B_BANK, :], ACT.Copy).then_inc(b_copied, 1)

            def operands(c, b, s):
                copy_b(c, s)
                if s == 0:
                    act.wait_ge(dt_done, c + 1)
                for t in range(CT):
                    i = s * CT + t
                    v = c * (CT * ST) + i
                    act.wait_ge(scan_done, SCAN0 + v - RING + 1)
                    act.activation(decay[:, i % RING, :], dt[:, b, t, :], ACT.Exp,
                                   scale=neg_a[:, t, s:s + 1]).then_inc(decay_done, 1)

            def body(c, b, do_tail, do_pre, do_gcn):
                for s in range(ST):
                    for on, state_ in ahead(s, do_pre):
                        operands(c + on, (b + on) % 2, state_)
                    if do_pre:
                        pre(s, c + 1, 1 - b)

            for s in range(ST):
                pre(s, 0, 0)
            operands(0, 0, 0)
            operands(0, 0, 1)
            over_chunks(act, body)

        @block.vector
        def _(dve):
            dve.wait_ge(y_loaded, 16)
            nc.vector.tensor_copy(y_p[0], y_full).then_inc(y_split, 1)
            dve.wait_ge(y_split, 1)
            nc.vector.tensor_tensor(y_rest, y_full, y_p[0], ALU.subtract).then_inc(y_split, 1)
            dve.wait_ge(y_split, 2)
            nc.vector.tensor_copy(y_p[1], y_rest).then_inc(y_split, 1)
            dve.wait_ge(y_split, 3)
            nc.vector.tensor_tensor(y_rest, y_rest, y_p[1], ALU.subtract).then_inc(y_split, 1)
            dve.wait_ge(y_split, 4)
            nc.vector.tensor_copy(y_p[2], y_rest).then_inc(y_split, 1)

            def stat_group(g):
                first = PIECE * (g % GROUPS)
                for i in range(first, first + PIECE):
                    nc.vector.bn_stats(stats[:, i, :], x1[:, i, :]).then_inc(stat_done, 1)
                for i in range(PIECE):
                    dve.wait_ge(stat_done, g * PIECE + i + 1)
                    agg = nc.vector.bn_aggr(mv[:, first + i, :], stats[:, first + i, :])
                agg.then_inc(mv_done, 1)

            def nmr_group(g):
                at = slice(PIECE * (g % GROUPS), PIECE * (g % GROUPS + 1))
                scale = rstd
                dve.wait_ge(rstd_done, g + 1)
                if g >= GROUPS:
                    scale = rstd_s
                    nc.vector.tensor_scalar(rstd_s[:, at], rstd[:, at], H_SCALE, None, ALU.mult).then_inc(scaled_done, 1)
                    dve.wait_ge(scaled_done, g - GROUPS + 1)
                nc.vector.scalar_tensor_tensor(nmr[:, at], mv[:, at, 0], -1.0, scale[:, at],
                                               ALU.mult, ALU.mult).then_inc(nmr_done, 1)

            def x_stats(g):
                dve.wait_ge(x_loaded[g], 16)
                stat_group(g)

            x_stats(0)
            nmr_group(0)
            x_stats(1)
            for g in range(1, GROUPS):
                if g + 1 < GROUPS:
                    x_stats(g + 1)
                nmr_group(g)

            def mix(n):
                nc.vector.scalar_tensor_tensor(x1[:, bass.ds(n, 1), :], h1[:, bass.ds(n, 1), :], ALPHA,
                                               x1[:, bass.ds(n, 1), :], ALU.mult, ALU.add).then_inc(x_mixed, 1)

            def mask_group(half, q, first):
                for r in range(SLOTS):
                    tile = half * NT + q * SLOTS + r
                    dve.wait_ge(adj_loaded[r], 16 * (half * (NT // SLOTS) + q + 1))
                    if not (first and r < 2):
                        dve.wait_ge(sup_done, HC * (tile - 1))
                        dve.wait_ge(mag_done, tile - 1)
                    for k in range(HC):
                        dve.wait_ge(mask_done, HC * tile + k + 1)
                        nc.vector.tensor_tensor(masked[:, r % 2, k * CH:(k + 1) * CH], bank[:, 6 + (r + k) % 2, :],
                                                adj_ring[:, r, k * CH:(k + 1) * CH], ALU.mult).then_inc(prod_done, 1)
                        if half > 0 and first and r == 0:
                            for n in range(k * TPC, (k + 1) * TPC):
                                x1_tile(half - 1, n)
                    if not (first and r == 0):
                        add_magnitudes(tile - 1, (r - 1) % 2)
                    if half == 0 and not first:
                        mix((q - 1) * SLOTS + r)
                    if half > 0 and first and r % 2 == 0:
                        dve.wait_ge(x1_done, X1_0 + HT)
                        stat_group(GROUPS + r // 2)
                    if half > 0 and first and r >= 2:
                        nmr_group(GROUPS + r - 2)

            def add_magnitudes(tile, slot, width=VW):
                dve.wait_ge(mag_done, tile + 1)
                dve.wait_ge(abs_done, tile)
                nc.vector.tensor_tensor(abs_sum[:, 0:width], magnitude[:, slot, 0:width], abs_sum[:, 0:width],
                                        ALU.add).then_inc(abs_done, 1)

            def row_scales(half):
                dve.wait_ge(rows_done, half + 1)
                nc.vector.tensor_scalar(rinv[:], bank[:, 5, 0:HT], ROW_EPS, None, ALU.max).then_inc(rinv_step, 1)
                dve.wait_ge(rinv_step, 3 * half + 1)
                nc.vector.reciprocal(rinv[:], rinv[:]).then_inc(rinv_step, 1)
                dve.wait_ge(rinv_step, 3 * half + 2)
                nc.vector.tensor_scalar(rinv[:], rinv[:], 1.0 - ALPHA, None, ALU.mult).then_inc(rinv_step, 1)
                dve.wait_ge(rinv_step, 3 * half + 3)
                dve.wait_ge(x_mixed, NT)

            def x1_tile(half, n):
                k, i = divmod(n, TPC)
                if i == 0:
                    dve.wait_ge(turned, half * HC + k + 1)
                nc.vector.scalar_tensor_tensor(x1[:, half * HT + n, :], bank[:, k, i * P:(i + 1) * P],
                                               rinv[:, n:n + 1], x1[:, half * HT + n, :],
                                               ALU.mult, ALU.add).then_inc(x1_done, 1)

            for half in range(HALVES):
                if half > 0:
                    row_scales(half - 1)
                nc.vector.memset(abs_sum[:, 0:VW], 0.0).then_inc(abs_zeroed, 1)
                dve.wait_ge(abs_zeroed, half + 1)
                mask_group(half, 0, True)
                if half == 0:
                    dve.wait_ge(h0_loaded, 16)
                    dve.wait_ge(h0r_done, NT)
                with dve.Fori(1, NT // SLOTS) as q:
                    mask_group(half, q, False)
                if half == 0:
                    for n in range(NT - SLOTS, NT):
                        mix(n)
                dve.wait_ge(abs_pool_done, half * (NT + 1) + NT)
                add_magnitudes(half * NT + NT - 1, 1, VW_LAST)

            dve.wait_ge(low_checked, HALVES * NT)
            nc.vector.reduce_sum(low_row[:], low_sum[:], axis=mybir.AxisListType.X).then_inc(low_added, 1)

            def h_rest(pieces):
                for i in pieces:
                    dve.wait_ge(h_hi_done, i + 1)
                    nc.vector.tensor_tensor(h_lo[:, i * PIECE:(i + 1) * PIECE, :], h1[:, i * PIECE:(i + 1) * PIECE, :],
                                            h_hi[:, i * PIECE:(i + 1) * PIECE, :], ALU.subtract).then_inc(h_lo_done, 1)

            h_rest(range(GROUPS // 2))
            dve.wait_ge(low_total, 1)
            nc.vector.tensor_copy(low_all[:], bank[0:1, 6, 0:1]).then_inc(low_known, 1)

            def normalise(g):
                stat_group(GROUPS + g)
                nmr_group(GROUPS + g)

            row_scales(HALVES - 1)
            for n in range(HT):
                x1_tile(HALVES - 1, n)
                if (n + 1) % PIECE == 0:
                    dve.wait_ge(x1_done, X1_0 + NT - HT + n + 1)
                    normalise((NT - HT + n) // PIECE)
            h_rest(range(GROUPS // 2, GROUPS))

            def pre(step, k, pb):
                if step == 2:
                    dve.wait_ge(mean_done, k + 1)
                    nc.vector.tensor_tensor(centred, h_t, bank[:, M1, :], ALU.subtract).then_inc(centred_done, 1)
                if step == 4:
                    dve.wait_ge(rs_done, k + 1)
                    nc.vector.scalar_tensor_tensor(normed, centred, g_ln[:], log_var, ALU.mult,
                                                   ALU.mult).then_inc(normed_done, 1)
                if step in CONV_STEPS:
                    at = CONV_STEPS.index(step)
                    taps = CT * (KC - 1)
                    for n in range(taps * at // len(CONV_STEPS), taps * (at + 1) // len(CONV_STEPS)):
                        j, t = divmod(n, CT)
                        if j == 0:
                            dve.wait_ge(tap_done, CT * k + t + 1)
                        else:
                            dve.wait_ge(conv_step, taps * k + n - CT + 1)
                        nc.vector.scalar_tensor_tensor(conv_out[:, t, :], conv_in[:, t, j + 1:j + 1 + CH],
                                                       w_cv[:, t, j + 1:j + 2], conv_out[:, t, :],
                                                       ALU.mult, ALU.add).then_inc(conv_step, 1)
                if step == 14:
                    dve.wait_ge(dt_log_step, 2 * (k + 1))
                    dve.wait_ge(dt_pos_done, CT * (k + 1))
                    nc.vector.tensor_tensor(dt[:, pb], dt_pos, dt_abs, ALU.add).then_inc(dt_done, 1)

            def tail(step, c, b):
                if step == 1:
                    if isinstance(c, int) and c == NC - 1:
                        dve.wait_ge(u_done, NC)
                        dve.wait_ge(o_done, NC - 1)
                    else:
                        dve.wait_ge(u_done, c + 2)
                    for t in range(CT):
                        dve.wait_ge(sum_done, SUM0 + summed_before(c, CT * ST) - CT + t + 1)
                        nc.vector.scalar_tensor_tensor(y_gated[:, t, :], u[:, b, t, :], d_sk[:, t:t + 1],
                                                       bank[:, Y_BANK + t, :], ALU.mult, ALU.add).then_inc(y_mix, 1)
                if step == 2:
                    dve.wait_ge(y_mix, CT * (c + 1))
                    nc.vector.tensor_tensor(y_gated, y_gated, z_gate[:, b], ALU.mult).then_inc(y_gate, 1)
                if step == OUT_STEP + 1:
                    dve.wait_ge(o_done, c + 1)
                    dve.wait_ge(stored, STORED0 + 16 * c)
                    nc.vector.tensor_tensor(x_out, bank[:, M1, :].rearrange("p (n d) -> p n d", d=D),
                                            x1[:, bass.ds(c * TPC, TPC), :], ALU.add).then_inc(xo_done, 1)

            def body(c, b, do_tail, do_pre, do_gcn):
                def times_c(i):
                    v = c * (CT * ST) + i
                    dve.wait_ge(c_done, c * ST + i // CT + 1)
                    dve.wait_ge(scan_done, SCAN0 + v + 1)
                    freed = i - SUM_RING + 1
                    if ((i - SUM_RING) // CT) % ST + 1 in POOL_PAIRED:
                        freed += CT
                    dve.wait_ge(sum_done, SUM0 + summed_before(c, freed))
                    nc.vector.tensor_tensor(state_c[:, i % SUM_RING, :], state[:, i % STATE_RING, :],
                                            bank[:, C_BANK + (i // CT) % 2, :], ALU.mult).then_inc(sc_done, 1)

                def pair_up(i):
                    if i // CT in paired(c, DVE_PAIRED):
                        dve.wait_ge(sc_done, SC0 + c * (CT * ST) + i + 1)
                        nc.vector.tensor_tensor(state_c[:, i % SUM_RING, :], state_c[:, i % SUM_RING, :],
                                                state_c[:, (i - CT) % SUM_RING, :], ALU.add).then_inc(paired_done, 1)

                for s in range(ST):
                    for t in range(CT):
                        i = s * CT + t
                        v = c * (CT * ST) + i
                        dve.wait_ge(decay_done, v + 1)
                        dve.wait_ge(drive_done, DRIVE0 + v + 1)
                        dve.wait_ge(carried, CARRY0 + v - STATE_RING + 1)
                        nc.vector.tensor_tensor_scan(state[:, i % STATE_RING, :], decay[:, i % RING, :],
                                                     drive[:, i % RING, :], carry[:, i:i + 1],
                                                     ALU.mult, ALU.add).then_inc(scan_done, 1)
                        if i > 0:
                            times_c(i - 1)
                        if i > 1:
                            pair_up(i - 2)
                    if do_tail:
                        tail(s, c - 1, 1 - b)
                    if do_pre:
                        pre(s, c + 1, 1 - b)
                times_c(CT * ST - 1)
                pair_up(CT * ST - 2)
                pair_up(CT * ST - 1)

            for s in range(ST):
                pre(s, 0, 0)
            over_chunks(dve, body)
            for s in range(ST):
                tail(s, NC - 1, (NC - 1) % 2)


def kernel(x, adj, L0_gnn_h0, L0_gnn_y, L1_gnn_gcn_w, L1_gnn_gcn_b, L1_gnn_ln_g, L1_gnn_ln_b, L1_gnn_w_in,
           L1_gnn_conv_w, L1_gnn_conv_b, L1_gnn_w_xp, L1_gnn_w_dt, L1_gnn_b_dt, L1_gnn_A_log, L1_gnn_D_skip,
           L1_gnn_w_out):
    import numpy as np
    import concourse.bacc as bacc
    from concourse.bass_utils import run_bass_kernel_spmd

    def rows(a):
        a = np.asarray(a)
        return np.concatenate([a, np.zeros((NP - N,) + a.shape[1:], a.dtype)])

    def columns(a):
        return np.ascontiguousarray(np.asarray(a).reshape(-1, P).T)

    adj_t = np.zeros((NP, NP), np.asarray(adj).dtype)
    adj_t[:N, :N] = np.asarray(adj).T
    y_t = np.ascontiguousarray(rows(L0_gnn_y).T)
    arrays = [("x", rows(x)), ("h0", rows(L0_gnn_h0)), ("adj_t", adj_t), ("y_t", y_t),
              ("gcn_w", L1_gnn_gcn_w), ("gcn_b", columns(L1_gnn_gcn_b)), ("ln_g", columns(L1_gnn_ln_g)),
              ("ln_b", columns(L1_gnn_ln_b)), ("w_in", L1_gnn_w_in), ("conv_w", L1_gnn_conv_w),
              ("conv_b", columns(L1_gnn_conv_b)), ("w_xp", L1_gnn_w_xp), ("w_dt", L1_gnn_w_dt),
              ("b_dt", columns(L1_gnn_b_dt)), ("a_log", L1_gnn_A_log), ("d_skip", columns(L1_gnn_D_skip)),
              ("w_out", L1_gnn_w_out)]
    nc = bacc.Bacc("TRN2", target_bir_lowering=False, num_devices=1)
    feed, args = {}, []
    for name, a in arrays:
        a = np.ascontiguousarray(a)
        feed[f"in_{name}"] = a
        args.append(nc.dram_tensor(f"in_{name}", a.shape, mybir.dt.from_np(a.dtype), kind="ExternalInput").ap())
    out = nc.dram_tensor("out_x", (N, D), F32, kind="ExternalOutput").ap()
    build(nc, *args, out)
    r = run_bass_kernel_spmd(nc, [feed], core_ids=[0])
    return r.results[0]["out_x"]
```
